# Optimizing a Trainium2 kernel written in Bass

```python
import numpy as np
import jax
import jax.numpy as jnp

def _softmax(x, axis=-1):
    return jax.nn.softmax(x, axis=axis)

def _gelu(x):
    return jax.nn.gelu(x, approximate=True)

def _silu(x):
    return jax.nn.silu(x)

def _sigmoid(x):
    return jax.nn.sigmoid(x)

def _layernorm(x, axis=-1, eps=1e-05):
    m = jnp.mean(x, axis=axis, keepdims=True)
    v = jnp.var(x, axis=axis, keepdims=True)
    return (x - m) / jnp.sqrt(v + eps)

def _scatter_add(tgt, idx, src, axis=0):
    return tgt.at[idx].add(src)

def _segment_sum(src, seg, n):
    return jax.ops.segment_sum(src, seg, n)
kernel_name = 'mk_audio_tower_d1_tok_audfeat256_r4_7dd29d'

def setup_inputs(seed: int=0):
    np.random.seed(seed)
    _w = jnp.asarray

    def _rec_inputs():
        import jax
        import jax.numpy as jnp
        _rk = jax.random.key(seed)
        x = -5.07413e-05 + 0.999912 * jax.random.normal(jax.random.fold_in(_rk, 1), (16, 256, 64), jnp.float32)
        return x
    x = _rec_inputs()

    def _L0_tok_setup():
        import jax, jax.numpy as jnp
        from jax import lax
        import numpy as np
        B, T, C, K, STRIDE = (16, 4000, 64, 5, 2)
        EPS = 0.001
        key = jax.random.key(seed)
        k0, k1, k2, k3 = jax.random.split(key, 4)
        x = jax.random.normal(k0, (B, T, C), dtype=jnp.float32)
        w = jax.random.normal(k1, (K, 1, C), dtype=jnp.float32) * 0.1
        b = jax.random.normal(k2, (C,), dtype=jnp.float32) * 0.01
        gamma = jnp.ones((C,), dtype=jnp.float32)
        beta = jnp.zeros((C,), dtype=jnp.float32)
        alpha = jnp.full((C,), 0.25, dtype=jnp.float32) + 0.01 * jax.random.normal(k3, (C,), dtype=jnp.float32)
        return {'x': x, 'w': w, 'b': b, 'gamma': gamma, 'beta': beta, 'alpha': alpha}
    _L0_tok_all = _L0_tok_setup()
    _L0_tok_in = {k: v for k, v in _L0_tok_all.items() if k in ('w', 'b', 'gamma', 'beta', 'alpha')}
    del _L0_tok_all

    def _L0_attn_setup():
        import jax, jax.numpy as jnp
        import numpy as np
        D_MODEL = 64
        N_HEAD = 8

        def _l1_scores(q, k):
            scale = 1.0 / np.sqrt(q.shape[-1]).astype(np.float32)
            q_sbhw = q.transpose(1, 0, 2, 3)

            def one_query(qs):
                return -jnp.sum(jnp.abs(qs[:, None, :, :] - k), axis=-1) * scale
            s = jax.lax.map(one_query, q_sbhw)
            return s.transpose(1, 0, 2, 3)
        key = jax.random.key(seed)
        ks = jax.random.split(key, 3)
        b, t = (4, 250)
        x = jax.random.normal(ks[0], (b, t, D_MODEL), jnp.float32)
        wqv_w = 0.005 * jax.random.normal(ks[1], (3 * N_HEAD * D_MODEL, D_MODEL), jnp.float32)
        wqv_b = jnp.zeros((3 * N_HEAD * D_MODEL,), jnp.float32)
        wk = 0.005 * jnp.ones((N_HEAD, D_MODEL), jnp.float32)
        fanin_w = 0.005 * jax.random.normal(ks[2], (D_MODEL, D_MODEL), jnp.float32)
        fanin_b = jnp.zeros((D_MODEL,), jnp.float32)
        return dict(x=x, wqv_w=wqv_w, wqv_b=wqv_b, wk=wk, fanin_w=fanin_w, fanin_b=fanin_b)
    _L0_attn_all = _L0_attn_setup()
    _L0_attn_in = {k: v for k, v in _L0_attn_all.items() if k in ('wqv_w', 'wqv_b', 'wk', 'fanin_w', 'fanin_b')}
    del _L0_attn_all

    def _L0_ffn_setup():
        import jax, jax.numpy as jnp
        import numpy as np
        E, D, H, TOP_K = (6, 64, 64, 2)
        ROUTER_H = D // 2
        key = jax.random.key(seed)
        ks = jax.random.split(key, 12)
        s = 1.0 / np.sqrt(D)
        sh = 1.0 / np.sqrt(H)
        sr = 1.0 / np.sqrt(ROUTER_H)
        return {'features': jax.random.normal(ks[0], (8, 1024, D), dtype=jnp.float32), 'router_w1': jax.random.uniform(ks[1], (D, ROUTER_H), jnp.float32, -s, s), 'router_b1': jnp.zeros((ROUTER_H,), jnp.float32), 'router_w2': jax.random.uniform(ks[2], (ROUTER_H, E), jnp.float32, -sr, sr), 'router_b2': jnp.zeros((E,), jnp.float32), 'expert_w1': jax.random.uniform(ks[3], (E, D, H), jnp.float32, -s, s), 'expert_b1': jnp.zeros((E, H), jnp.float32), 'expert_w2': jax.random.uniform(ks[4], (E, H, H), jnp.float32, -sh, sh), 'expert_b2': jnp.zeros((E, H), jnp.float32), 'expert_w3': jax.random.uniform(ks[5], (E, H, D), jnp.float32, -sh, sh), 'expert_b3': jnp.zeros((E, D), jnp.float32)}
    _L0_ffn_all = _L0_ffn_setup()
    _L0_ffn_in = {k: v for k, v in _L0_ffn_all.items() if k in ('router_w1', 'router_b1', 'router_w2', 'router_b2', 'expert_w1', 'expert_b1', 'expert_w2', 'expert_b2', 'expert_w3', 'expert_b3')}
    del _L0_ffn_all
    return {'x': x, 'L0_tok_w': _L0_tok_in['w'], 'L0_tok_b': _L0_tok_in['b'], 'L0_tok_gamma': _L0_tok_in['gamma'], 'L0_tok_beta': _L0_tok_in['beta'], 'L0_tok_alpha': _L0_tok_in['alpha'], 'L0_attn_wqv_w': _L0_attn_in['wqv_w'], 'L0_attn_wqv_b': _L0_attn_in['wqv_b'], 'L0_attn_wk': _L0_attn_in['wk'], 'L0_attn_fanin_w': _L0_attn_in['fanin_w'], 'L0_attn_fanin_b': _L0_attn_in['fanin_b'], 'L0_ffn_router_w1': _L0_ffn_in['router_w1'], 'L0_ffn_router_b1': _L0_ffn_in['router_b1'], 'L0_ffn_router_w2': _L0_ffn_in['router_w2'], 'L0_ffn_router_b2': _L0_ffn_in['router_b2'], 'L0_ffn_expert_w1': _L0_ffn_in['expert_w1'], 'L0_ffn_expert_b1': _L0_ffn_in['expert_b1'], 'L0_ffn_expert_w2': _L0_ffn_in['expert_w2'], 'L0_ffn_expert_b2': _L0_ffn_in['expert_b2'], 'L0_ffn_expert_w3': _L0_ffn_in['expert_w3'], 'L0_ffn_expert_b3': _L0_ffn_in['expert_b3']}

def reference(x, L0_tok_w, L0_tok_b, L0_tok_gamma, L0_tok_beta, L0_tok_alpha, L0_attn_wqv_w, L0_attn_wqv_b, L0_attn_wk, L0_attn_fanin_w, L0_attn_fanin_b, L0_ffn_router_w1, L0_ffn_router_b1, L0_ffn_router_w2, L0_ffn_router_b2, L0_ffn_expert_w1, L0_ffn_expert_b1, L0_ffn_expert_w2, L0_ffn_expert_b2, L0_ffn_expert_w3, L0_ffn_expert_b3):
    import jax
    import jax.numpy as jnp

    def _L0_tok_ref(x, w, b, gamma, beta, alpha):
        import jax, jax.numpy as jnp
        from jax import lax
        import numpy as np
        B, T, C, K, STRIDE = (16, 4000, 64, 5, 2)
        EPS = 0.001
        y = lax.conv_general_dilated(x, w, window_strides=(STRIDE,), padding='SAME', dimension_numbers=('NWC', 'WIO', 'NWC'), feature_group_count=C) + b
        mean = jnp.mean(y, axis=(1, 2), keepdims=True)
        var = jnp.var(y, axis=(1, 2), keepdims=True)
        yn = (y - mean) * lax.rsqrt(var + EPS) * gamma + beta
        return jnp.where(yn > 0, yn, alpha * yn)

    def _L0_attn_ref(x, wqv_w, wqv_b, wk, fanin_w, fanin_b):
        import jax, jax.numpy as jnp
        import numpy as np
        D_MODEL = 64
        N_HEAD = 8

        def _l1_scores(q, k):
            scale = 1.0 / np.sqrt(q.shape[-1]).astype(np.float32)
            q_sbhw = q.transpose(1, 0, 2, 3)

            def one_query(qs):
                return -jnp.sum(jnp.abs(qs[:, None, :, :] - k), axis=-1) * scale
            s = jax.lax.map(one_query, q_sbhw)
            return s.transpose(1, 0, 2, 3)
        b, t, d = x.shape
        h = N_HEAD
        v = (x @ wqv_w.T + wqv_b).reshape(b, t, 3 * h, d)
        q, vf, vb = (v[:, :, :h], v[:, :, h:2 * h], v[:, :, 2 * h:])
        k = x[:, :, None, :] * wk[None, None]
        a = _l1_scores(q, k)
        a = jnp.concatenate([a, jnp.zeros((b, 1, t, h), a.dtype)], axis=1)
        a = jax.nn.softmax(a, axis=1)[:, :t]
        bf = jnp.einsum('bsdh,bshw->bdhw', a, vf)
        bb = jnp.einsum('bdsh,bshw->bdhw', a, vb)
        o = (bf + bb).sum(axis=2).reshape(b, t, d)
        y = o * jax.nn.sigmoid(1.702 * o)
        y = y @ fanin_w.T + fanin_b
        return x + y

    def _L0_ffn_ref(features, router_w1, router_b1, router_w2, router_b2, expert_w1, expert_b1, expert_w2, expert_b2, expert_w3, expert_b3):
        import jax, jax.numpy as jnp
        import numpy as np
        E, D, H, TOP_K = (6, 64, 64, 2)
        ROUTER_H = D // 2
        rh = jax.nn.relu(features @ router_w1 + router_b1)
        expert_logits = jax.nn.softmax(rh @ router_w2 + router_b2, axis=-1)
        top_w, top_i = jax.lax.top_k(expert_logits, TOP_K)
        routing_weights = jax.nn.softmax(top_w, axis=-1)
        h1 = jax.nn.relu(jnp.einsum('bsd,edh->bseh', features, expert_w1) + expert_b1)
        h2 = jax.nn.relu(jnp.einsum('bseh,ehf->bsef', h1, expert_w2) + expert_b2)
        expert_out = jnp.einsum('bsef,efo->bseo', h2, expert_w3) + expert_b3
        sel = jnp.take_along_axis(expert_out, top_i[:, :, :, None], axis=2)
        combined = jnp.sum(sel * routing_weights[..., None], axis=2)
        return combined
    h = _L0_tok_ref(x, L0_tok_w, L0_tok_b, L0_tok_gamma, L0_tok_beta, L0_tok_alpha)
    h = h + _L0_attn_ref(_layernorm(h, axis=-1), L0_attn_wqv_w, L0_attn_wqv_b, L0_attn_wk, L0_attn_fanin_w, L0_attn_fanin_b)
    h = h + _L0_ffn_ref(_layernorm(h, axis=-1), L0_ffn_router_w1, L0_ffn_router_b1, L0_ffn_router_w2, L0_ffn_router_b2, L0_ffn_expert_w1, L0_ffn_expert_b1, L0_ffn_expert_w2, L0_ffn_expert_b2, L0_ffn_expert_w3, L0_ffn_expert_b3)
    return h

_drawn_inputs = setup_inputs


def setup_inputs(seed=0):
    import zlib

    import numpy as np

    out = dict(_drawn_inputs(seed))
    spreads = {'L0_tok_gamma': (1.0, 0.2),
     'L0_tok_beta': (0.0, 0.1),
     'L0_attn_wqv_b': (0.0, 0.8),
     'L0_attn_wk': (0.004999999888241291, 0.6),
     'L0_attn_fanin_b': (0.0, 0.1),
     'L0_ffn_router_b1': (0.0, 0.329),
     'L0_ffn_router_b2': (0.0, 0.1),
     'L0_ffn_expert_b1': (0.0, 0.8),
     'L0_ffn_expert_b2': (0.0, 0.472),
     'L0_ffn_expert_b3': (0.0, 0.1)}
    factors = {'L0_tok_alpha': 3.797, 'L0_attn_wqv_w': 8.0, 'L0_attn_fanin_w': 8.0}
    for name, (base, spread) in spreads.items():
        noise = np.random.default_rng([zlib.crc32(name.encode()), seed]).standard_normal(out[name].shape)
        drawn = base * np.exp(spread * noise) if base else spread * noise
        out[name] = jnp.asarray(drawn.astype(out[name].dtype))
    for name, factor in factors.items():
        out[name] = (out[name] * factor).astype(out[name].dtype)
    return out
```

```python
from contextlib import ExitStack

import concourse.bass as bass
from concourse import mybir

F32 = mybir.dt.float32
ALU = mybir.AluOpType
ACT = mybir.ActivationFunctionType
AX = mybir.AxisListType

NB, T_IN, C = 16, 256, 64
TAPS = 5
T = T_IN // 2
NH = 8
P = 128
BG = 2
NG = NB // BG
GC = BG * T
TQ = 4
NJ = 32 // 2
HEADS_PER_BANK = 512 // GC
NE, RH = 6, 32
NP = NE // 2
TINY = 1e-30
CONV_EPS, LN_EPS = 1e-3, 1e-5
CHUNK_B = 4

COLS = {}
_at = 0
for _name, _n in [("ident", P), ("wq", 4 * 2 * C), ("wv", NH * C), ("wk", NH), ("bq", NH), ("fan", P),
                  ("w1", NE * C), ("w2", NP * P), ("w3", NP * C), ("rw1", RH), ("rw2", NE), ("b1", NP),
                  ("b2", NP), ("rb1", 1), ("b3", C), ("pick", NP * P)]:
    COLS[_name] = (_at, _at + _n)
    _at += _n
NCOLS = _at
ROWS = {}
_at = 0
for _name, _n in [("conv_w", TAPS * C), ("conv_b", C), ("gamma", C), ("beta", C), ("alpha", C), ("fan_b", C),
                  ("bv", 2 * NH * C), ("rb2", NE), ("lower", NE * NE)]:
    ROWS[_name] = (_at, _at + _n)
    _at += _n
NROWS = _at


def build(nc, x_pad, cols, rows, out):
    with ExitStack() as ctx:
        def sb(name, shape):
            return ctx.enter_context(nc.sbuf_tensor(name, shape, F32))

        def sem(name):
            return ctx.enter_context(nc.semaphore(name))

        const = sb("const", [P, NCOLS])
        row = sb("row", [P, NROWS])
        x5 = sb("x5", [P, NB, TAPS, C])
        h = sb("h", [P, NB, C])
        base = sb("base", [P, NB, C])
        xn2x = sb("xn2x", [P, NB, 2, C])
        tmp = sb("tmp", [P, NB, C])
        tmp2 = sb("tmp2", [P, NB, C])
        small = sb("small", [P, 8, NB])
        ones = sb("ones", [P, P])
        XT = sb("XT", [P, NB, T])
        x_now = sb("x_now", [P, BG, T])
        x_next = sb("x_next", [P, BG, T])
        neg_x = sb("neg_x", [P, NB, NJ, TQ])
        neg_xw = sb("neg_xw", [P, NB, NH])
        abs_wk = sb("abs_wk", [P, NH])
        sgn_wk = sb("sgn_wk", [P, NH])
        inv_wk = sb("inv_wk", [P, NH])
        wk8 = sb("wk8", [P, NH])
        start_w = sb("start_w", [P, NH, P])
        hot = sb("hot", [P, NH, 62])
        window = sb("window", [P, 2, NH, 32])
        qn = sb("qn", [P, NH, BG, T])
        D = sb("D", [P, 2, TQ, NH * GC])
        V = sb("V", [P, BG, 2, NH * C])
        A = sb("A", [P, NH, BG, T])
        AT = sb("AT", [P, NH, BG, T])
        den = sb("den", [P, NH, BG])
        den1 = sb("den1", [P, NH, BG])
        rden = sb("rden", [P, NH, BG])
        OT = sb("OT", [P, NG, T])
        ps = ctx.enter_context(nc.psum_tensor("ps", [P, 8, 512], F32))
        R = ps[:, 0:4, :].rearrange("p k (h n) -> p (k h) n", n=GC)

        def cst(name):
            a, b = COLS[name]
            return const[:, a:b]

        def rw(name):
            a, b = ROWS[name]
            return row[:, a:b]

        ident = cst("ident")
        wq = cst("wq").rearrange("p (m n) -> p m n", m=4)
        wv = cst("wv")
        Dt = D[:, 0, :, :].rearrange("p g n -> p (g n)")
        Du = D[:, 1, :, :].rearrange("p g n -> p (g n)")
        gate = Dt[:, 0:1024]
        yT = Dt[:, 1024:2048].rearrange("p (g t) -> p g t", g=NG)
        X2T = Dt[:, 2048:3072].rearrange("p (g t) -> p g t", g=NG)
        rhT = Dt[:, 3072:5120].rearrange("p (i g t) -> p i g t", i=2, g=NG)
        cwT = Dt[:, 5120:7168].rearrange("p (i g t) -> p i g t", i=2, g=NG)
        H1 = Du[:, 0:1024].rearrange("p (k n) -> p k n", k=2)
        H2 = Du[:, 1024:2048].rearrange("p (k n) -> p k n", k=2)
        H2c = Du[:, 2048:3072].rearrange("p (k n) -> p k n", k=2)
        result = Du[:, 3072:4096].rearrange("p (b c) -> p b c", b=NB)
        rt = Du[:, 4096:4096 + 8 * 96].rearrange("p (k b e) -> p k b e", k=8, e=NE)
        rank6 = Du[:, 5120:5120 + 2 * 576].rearrange("p (k b e f) -> p k b e f", k=2, b=NB, e=NE)

        const_loaded, rows_loaded = sem("const_loaded"), sem("rows_loaded")
        x_loaded = [sem(f"x_loaded{i}") for i in range(NB // CHUNK_B)]
        dve_step = sem("dve_step")
        pool_step = sem("pool_step")
        wk_ready = sem("wk_ready")
        stat_ready, stat_summed = sem("stat_ready"), sem("stat_summed")
        act_in, act_out = sem("act_in"), sem("act_out")
        xn_ready, xt_psum, xt_ready = sem("xn_ready"), sem("xt_psum"), sem("xt_ready")
        neg_x_ready = sem("neg_x_ready")
        xw_psum, xw_ready = sem("xw_psum"), sem("xw_ready")
        base_ready = sem("base_ready")
        x_copied = sem("x_copied")
        qp_ready = sem("qp_ready")
        q_ready = sem("q_ready")
        vp_ready, v_ready = sem("vp_ready"), sem("v_ready")
        win_ready = sem("win_ready")
        dve_half, act_half = sem("dve_half"), sem("act_half")
        half_free = sem("half_free")
        e_ready = sem("e_ready")
        norm_step = sem("norm_step")
        a_ready = sem("a_ready")
        tp_ready, at_ready = sem("tp_ready"), sem("at_ready")
        o_done, o_saved = sem("o_done"), sem("o_saved")
        y_ready, fan_done = sem("y_ready"), sem("fan_done")
        x2_ready, x2t_psum, x2t_ready = sem("x2_ready"), sem("x2t_psum"), sem("x2t_ready")
        rh_psum, rh_ready, logit_psum = sem("rh_psum"), sem("rh_ready"), sem("logit_psum")
        cw_ready, cwt_psum, cwt_ready = sem("cw_ready"), sem("cwt_psum"), sem("cwt_ready")
        h1_psum, h1_ready = sem("h1_psum"), sem("h1_ready")
        h2_psum, h2_ready = sem("h2_psum"), sem("h2_ready")
        h2c_ready = sem("h2c_ready")
        y_psum, result_ready, stored = sem("y_psum"), sem("result_ready"), sem("stored")

        NHALF = 2 * NJ // 2
        BANKS = 4
        ACT_PIECES = ((0, 1), (2, 1), (3, 1))
        CHUNKS = [(i, g) for g in range(0, NG, CHUNK_B) for i in range(2)]
        UNITS = [(n, p) for n in range(len(CHUNKS)) for p in range(NP)]

        block = ctx.enter_context(nc.Block())

        @block.sync
        def _(sp):
            for k in range(NB // CHUNK_B):
                b = slice(k * CHUNK_B, (k + 1) * CHUNK_B)
                for first, n in ((0, 2), (2, 2), (4, 1)):
                    src = x_pad[b, first:first + T_IN, :].rearrange("b (t r) c -> t b r c", r=2)[:, :, 0:n, :]
                    sp.dma_start(x5[:, b, first:first + n, :], src).then_inc(x_loaded[k], 16)
            for n, (i, g) in enumerate(CHUNKS):
                sp.wait_ge(result_ready, n + 1)
                view = out.rearrange("(g i) t c -> i t g c", i=2)[i, :, g:g + CHUNK_B, :]
                mine = result.rearrange("p (g i) c -> p i g c", i=2)[:, i, g:g + CHUNK_B, :]
                sp.dma_start(view, mine).then_inc(stored, 16)
            sp.wait_ge(stored, 16 * len(CHUNKS))

        @block.gpsimd
        def _(pool):
            steps = [0]

            def step(ins):
                steps[0] += 1
                ins.then_inc(pool_step, 1)
                pool.wait_ge(pool_step, steps[0])

            step(nc.gpsimd.memset(ones[:], 1.0))
            step(nc.gpsimd.memset(hot[:], 0.0))
            pool.wait_ge(wk_ready, 1)
            step(nc.gpsimd.tensor_copy(hot[0:C, :, 30], abs_wk[0:C, :]))
            step(nc.gpsimd.tensor_copy(hot[C:P, :, 31], abs_wk[C:P, :]))
            step(nc.gpsimd.tensor_scalar(start_w[:], abs_wk[:].unsqueeze(2).to_broadcast([P, NH, P]), -0.25, None,
                                         ALU.mult))
            pool.wait_ge(xn_ready, 1)
            step(nc.gpsimd.tensor_tensor(base[:], h[:], xn2x[:, :, 0, :], ALU.add))
            nc.gpsimd.tensor_tensor(base[:], base[:], rw("fan_b").unsqueeze(1).to_broadcast([P, NB, C]),
                                    ALU.add).then_inc(base_ready, 1)

            def group(G, last):
                pool.wait_ge(vp_ready, G * BG + BG)
                flat = XT[:].rearrange("p b t -> p (b t)")
                copy = nc.gpsimd.tensor_copy(x_now[:].rearrange("p b t -> p (b t)"), flat[:, bass.ds(G * GC, GC)])
                if not last:
                    copy = nc.gpsimd.tensor_copy(x_next[:].rearrange("p b t -> p (b t)"),
                                                 flat[:, bass.ds(G * GC + GC, GC)])
                copy.then_inc(x_copied, 1)
                with pool.Fori(0, NJ // 2) as J:
                    for half in range(2):
                        pool.wait_ge(half_free, G * NHALF + J * 2 + (half + 1))
                        nc.gpsimd.tensor_copy(window[:, half, :, :],
                                              hot[:, :, bass.ds(J * -4 + (30 - 2 * half), 32)]).then_inc(win_ready, 1)

            pool.wait_ge(xt_ready, 4)
            with pool.Fori(0, NG - 1) as G:
                group(G, False)
            group(NG - 1, True)

        def relu_piece(engine, G, J, half, g, b):
            dst = D[:, half, g, :].rearrange("p (h b t) -> p h b t", h=NH, b=BG)[:, :, b, :]
            minus_x = neg_x[:].rearrange("p b j g -> p (b j g)")[
                :, bass.ds(G * (BG * NJ * TQ) + J * (2 * TQ) + (b * NJ * TQ + half * TQ + g), 1)]
            if engine is nc.scalar:
                return nc.scalar.activation(dst, qn[:, :, b, :], ACT.Relu, bias=minus_x)
            return nc.vector.tensor_scalar(dst, qn[:, :, b, :], minus_x, 0.0, ALU.add, ALU.max)

        PIECES = [(g, b) for g in range(TQ) for b in range(BG)]

        @block.scalar
        def _(act):
            act.dma_start(const[:], cols).then_inc(const_loaded, 16)
            act.dma_start(row[:], rows.partition_broadcast(P)).then_inc(rows_loaded, 16)

            act.wait_ge(act_in, 1)
            nc.scalar.activation(tmp2[:], tmp[:], ACT.Square).then_inc(act_out, 1)
            act.wait_ge(act_in, 2)
            nc.scalar.activation(small[:, 2, :], small[:, 1, :], ACT.Sqrt).then_inc(act_out, 1)
            act.wait_ge(act_in, 3)
            nc.scalar.activation(tmp2[:], tmp[:], ACT.Relu).then_inc(act_out, 1)
            act.wait_ge(act_in, 4)
            nc.scalar.activation(tmp2[:], tmp[:], ACT.Square).then_inc(act_out, 1)
            act.wait_ge(act_in, 5)
            nc.scalar.activation(small[:, 2, :], small[:, 1, :], ACT.Sqrt).then_inc(act_out, 1)
            for k in range(4):
                act.wait_ge(xt_psum, k + 1)
                nc.scalar.activation(XT[:, 4 * k:4 * k + 4, :],
                                     ps[:, k, :].rearrange("p (b t) -> p b t", b=4), ACT.Copy).then_inc(xt_ready, 1)

            def group(G, last):
                act.wait_ge(q_ready, G * 2 + 2)
                with act.Fori(0, NJ // 2) as J:
                    for half in range(2):
                        act.wait_ge(half_free, G * NHALF + J * 2 + (half + 1))
                        for g, b in ACT_PIECES:
                            piece = relu_piece(nc.scalar, G, J, half, g, b)
                        piece.then_inc(act_half, 1)
                act.wait_ge(half_free, G * NHALF + (NHALF + 2))
                for k in range(BANKS):
                    for hd in range(HEADS_PER_BANK * k, HEADS_PER_BANK * (k + 1)):
                        for b in range(BG):
                            e = nc.scalar.activation(
                                A[:, hd, b, :], R[:, hd, b * T:(b + 1) * T], ACT.Exp, scale=-0.25,
                                bias=neg_xw[:].rearrange("p b h -> p (b h)")[:, bass.ds(G * (BG * NH) + (b * NH + hd), 1)],
                                accum_out=den[:, hd, b:b + 1])
                    e.then_inc(e_ready, 1)
                for k in range(BANKS):
                    act.wait_ge(tp_ready, G * BANKS + (k + 1))
                    nc.scalar.activation(AT[:, 2 * k:2 * k + 2, :, :],
                                         ps[:, 4 + k % 2, :].rearrange("p (h b t) -> p h b t", h=2, b=BG),
                                         ACT.Copy).then_inc(at_ready, 1)

            act.wait_ge(xw_ready, 1)
            act.wait_ge(neg_x_ready, 8)
            with act.Fori(0, NG - 1) as G:
                group(G, False)
            group(NG - 1, True)

            act.wait_ge(o_saved, NG)
            nc.scalar.activation(gate, OT[:].rearrange("p g t -> p (g t)"), ACT.Exp, scale=-1.702).then_inc(act_out, 1)
            act.wait_ge(act_in, 6)
            nc.scalar.activation(tmp2[:], tmp[:], ACT.Square).then_inc(act_out, 1)
            act.wait_ge(act_in, 7)
            nc.scalar.activation(small[:, 2, :], small[:, 1, :], ACT.Sqrt).then_inc(act_out, 1)
            for k in range(2):
                act.wait_ge(x2t_psum, k + 1)
                nc.scalar.activation(X2T[:, 4 * k:4 * k + 4, :],
                                     ps[:, k, :].rearrange("p (g t) -> p g t", g=4), ACT.Copy).then_inc(x2t_ready, 1)
            for n, (i, g) in enumerate(CHUNKS):
                act.wait_ge(rh_psum, n + 1)
                nc.scalar.activation(rhT[0:RH, i, g:g + CHUNK_B, :],
                                     ps[0:RH, 2 + n, :].rearrange("p (g t) -> p g t", g=CHUNK_B),
                                     ACT.Relu, bias=cst("rb1")[0:RH, :]).then_inc(rh_ready, 1)
            act.wait_ge(act_in, 8)
            nc.scalar.activation(rt[:, 1], rt[:, 0], ACT.Exp).then_inc(act_out, 1)
            act.wait_ge(act_in, 9)
            nc.scalar.activation(rt[:, 3], rt[:, 2], ACT.Exp).then_inc(act_out, 1)
            for k in range(4):
                act.wait_ge(cwt_psum, k + 1)
                nc.scalar.activation(cwT[0:NE, :, :, :].rearrange("p i g t -> p (i g t)")[:, 512 * k:512 * k + 512],
                                     ps[0:NE, k, :], ACT.Copy).then_inc(cwt_ready, 1)
            for u, (n, p) in enumerate(UNITS):
                act.wait_ge(h1_psum, u + 1)
                if u >= 2:
                    act.wait_ge(h2_psum, u - 1)
                nc.scalar.activation(H1[:, u % 2, :], ps[:, u % 2, :], ACT.Relu,
                                     bias=cst("b1")[:, p:p + 1]).then_inc(h1_ready, 1)
                act.wait_ge(h2_psum, u + 1)
                if u >= 2:
                    act.wait_ge(h2c_ready, u - 1)
                nc.scalar.activation(H2[:, u % 2, :], ps[:, 2 + u % 2, :], ACT.Relu,
                                     bias=cst("b2")[:, p:p + 1]).then_inc(h2_ready, 1)

        @block.vector
        def _(dve):
            steps = [0]

            def step(ins):
                steps[0] += 1
                ins.then_inc(dve_step, 1)
                dve.wait_ge(dve_step, steps[0])

            def over_c(ap):
                return ap.unsqueeze(2).to_broadcast([P, NB, C])

            def over_b(ap):
                return ap.unsqueeze(1).to_broadcast([P, NB, C])

            dve.wait_ge(const_loaded, 16)
            step(nc.vector.tensor_scalar(inv_wk[:], cst("wk"), -1.0, None, ALU.mult))
            step(nc.vector.tensor_tensor(abs_wk[:], cst("wk"), inv_wk[:], ALU.max))
            step(nc.vector.tensor_scalar(abs_wk[:], abs_wk[:], TINY, None, ALU.max))
            step(nc.vector.tensor_scalar(sgn_wk[:], cst("wk"), 0.0, 2.0, ALU.is_ge, ALU.mult))
            step(nc.vector.tensor_scalar(sgn_wk[:], sgn_wk[:], -1.0, None, ALU.add))
            step(nc.vector.reciprocal(inv_wk[:], abs_wk[:]))
            step(nc.vector.tensor_tensor(inv_wk[:], inv_wk[:], sgn_wk[:], ALU.mult))
            nc.vector.tensor_scalar(wk8[:], abs_wk[:], -0.125, None, ALU.mult).then_inc(wk_ready, 1)

            dve.wait_ge(rows_loaded, 16)
            for k in range(NB // CHUNK_B):
                b = slice(k * CHUNK_B, (k + 1) * CHUNK_B)
                dve.wait_ge(x_loaded[k], 48)
                flat = x5[:, b, :, :].rearrange("p b k c -> p b (k c)")
                step(nc.vector.tensor_tensor(flat, flat, rw("conv_w").unsqueeze(1).to_broadcast([P, CHUNK_B, TAPS * C]),
                                             ALU.mult))
                step(nc.vector.tensor_reduce(tmp[:, b, :], x5[:, b, :, :].rearrange("p b k c -> p b c k"),
                                             AX.X, ALU.add))
            step(nc.vector.tensor_tensor(tmp[:], tmp[:], over_b(rw("conv_b")), ALU.add))

            nc.vector.tensor_reduce(small[:, 0, :], tmp[:], AX.X, ALU.add).then_inc(stat_ready, 1)
            dve.wait_ge(stat_summed, 1)
            step(nc.vector.tensor_scalar(small[:, 3, :], ps[:, 0, 0:NB], 1.0 / (T * C), None, ALU.mult))
            nc.vector.tensor_tensor(tmp[:], tmp[:], over_c(small[:, 3, :]), ALU.subtract).then_inc(act_in, 1)
            dve.wait_ge(act_out, 1)
            nc.vector.tensor_reduce(small[:, 0, :], tmp2[:], AX.X, ALU.add).then_inc(stat_ready, 1)
            dve.wait_ge(stat_summed, 2)

            def root(source, scale, eps, turn):
                nc.vector.tensor_scalar(small[:, 1, :], source, scale, eps, ALU.mult, ALU.add).then_inc(act_in, 1)
                dve.wait_ge(act_out, turn)
                step(nc.vector.reciprocal(small[:, 3, :], small[:, 2, :]))
                step(nc.vector.tensor_tensor(small[:, 3, :], small[:, 3, :], small[:, 1, :], ALU.mult))
                step(nc.vector.tensor_tensor(small[:, 3, :], small[:, 3, :], small[:, 2, :], ALU.add))
                step(nc.vector.tensor_scalar(small[:, 3, :], small[:, 3, :], 0.5, None, ALU.mult))
                step(nc.vector.reciprocal(small[:, 5, :], small[:, 3, :]))

            root(ps[:, 0, NB:2 * NB], 1.0 / (T * C), CONV_EPS, 2)
            step(nc.vector.tensor_tensor(h[:], over_b(rw("gamma")), over_c(small[:, 5, :]), ALU.mult))
            step(nc.vector.tensor_tensor(tmp[:], tmp[:], h[:], ALU.mult))
            step(nc.vector.tensor_tensor(tmp[:], tmp[:], over_b(rw("beta")), ALU.add))
            nc.vector.tensor_scalar(h[:], tmp[:], 0.0, None, ALU.min).then_inc(act_in, 1)
            dve.wait_ge(act_in, 3)
            step(nc.vector.tensor_tensor(h[:], h[:], over_b(rw("alpha")), ALU.mult))
            dve.wait_ge(act_out, 3)
            step(nc.vector.tensor_tensor(h[:], h[:], tmp2[:], ALU.add))

            def layer_norm(source, turn):
                step(nc.vector.tensor_reduce(small[:, 0, :], source, AX.X, ALU.add))
                step(nc.vector.tensor_scalar(small[:, 4, :], small[:, 0, :], 1.0 / C, None, ALU.mult))
                nc.vector.tensor_tensor(tmp[:], source, over_c(small[:, 4, :]), ALU.subtract).then_inc(act_in, 1)
                dve.wait_ge(act_out, turn)
                step(nc.vector.tensor_reduce(small[:, 0, :], tmp2[:], AX.X, ALU.add))
                root(small[:, 0, :], 1.0 / C, LN_EPS, turn + 1)

            layer_norm(h[:], 4)
            nc.vector.tensor_tensor(xn2x[:, :, 0, :], tmp[:], over_c(small[:, 5, :]), ALU.mult)
            nc.vector.tensor_tensor(xn2x[:, :, 1, :], tmp[:], over_c(small[:, 5, :]), ALU.mult).then_inc(xn_ready, 1)

            for k in range(4):
                dve.wait_ge(xt_ready, k + 1)
                for parity in range(2):
                    half = slice(C * parity, C * parity + C)
                    src = XT[half, 4 * k:4 * k + 4, :].rearrange("p b (g j i) -> p i b j g", g=TQ, i=2)[:, parity, :, :, :]
                    for b in range(4):
                        ins = nc.vector.tensor_scalar(neg_x[half, 4 * k + b, :, :], src[:, b, :, :], -1.0, None,
                                                      ALU.mult)
                    ins.then_inc(neg_x_ready, 1)
            dve.wait_ge(xw_psum, 1)
            nc.vector.tensor_copy(neg_xw[:], ps[:, 4, 0:NB * NH].rearrange("p (b h) -> p b h", b=NB)).then_inc(xw_ready, 1)

            def save_q(G):
                for turn in range(2):
                    dve.wait_ge(qp_ready, G * 2 + (turn + 1))
                    for bank in range(2):
                        for k in range(2):
                            hd = 4 * bank + 2 * turn + k
                            ins = nc.vector.tensor_scalar(
                                qn[:, hd, :, :],
                                ps[:, 4 + 2 * turn + bank, k * GC:(k + 1) * GC].rearrange("p (b t) -> p b t", b=BG),
                                cst("bq")[:, hd:hd + 1], inv_wk[:, hd:hd + 1], ALU.add, ALU.mult)
                    ins.then_inc(q_ready, 1)

            def group(G, last):
                with dve.Fori(0, NJ // 2) as J:
                    dve.wait_ge(q_ready, G * 2 + 2)
                    for half in range(2):
                        dve.wait_ge(half_free, G * NHALF + J * 2 + (half + 1))
                        for g, b in PIECES:
                            if (g, b) not in ACT_PIECES:
                                piece = relu_piece(nc.vector, G, J, half, g, b)
                        piece.then_inc(dve_half, 1)
                if not last:
                    dve.wait_ge(act_half, G * NHALF + NHALF)
                    save_q(G + 1)
                for b in range(BG):
                    dve.wait_ge(vp_ready, G * BG + (BG + b + 1))
                    nc.vector.tensor_tensor(V[:, b, :, :], ps[:, 4 + 2 * b:6 + 2 * b, :],
                                            rw("bv").rearrange("p (d n) -> p d n", d=2), ALU.add).then_inc(v_ready, 1)
                for k in range(BANKS):
                    hs = slice(HEADS_PER_BANK * k, HEADS_PER_BANK * (k + 1))
                    dve.wait_ge(e_ready, G * BANKS + (k + 1))
                    nc.vector.tensor_scalar(den1[:, hs, :], den[:, hs, :], 1.0, None, ALU.add).then_inc(norm_step, 1)
                    dve.wait_ge(norm_step, G * (2 * BANKS) + (2 * k + 1))
                    nc.vector.reciprocal(rden[:, hs, :], den1[:, hs, :]).then_inc(norm_step, 1)
                    dve.wait_ge(norm_step, G * (2 * BANKS) + (2 * k + 2))
                    nc.vector.tensor_tensor(A[:, hs, :, :], A[:, hs, :, :],
                                            rden[:, hs, :].unsqueeze(3).to_broadcast([P, HEADS_PER_BANK, BG, T]),
                                            ALU.mult).then_inc(a_ready, 1)

            def save_o(G):
                dve.wait_ge(o_done, G + 1)
                nc.vector.tensor_copy(OT[:].rearrange("p g t -> p (g t)")[:, bass.ds(G * T, T)],
                                      ps[:, 6, 0:T]).then_inc(o_saved, 1)

            save_q(0)
            with dve.Fori(0, NG - 1) as G:
                group(G, False)
                save_o(G)
            group(NG - 1, True)
            save_o(NG - 1)

            dve.wait_ge(act_out, 6)
            step(nc.vector.tensor_scalar(gate, gate, 1.0, None, ALU.add))
            step(nc.vector.reciprocal(gate, gate))
            nc.vector.tensor_tensor(yT, OT[:], gate.rearrange("p (g t) -> p g t", g=NG), ALU.mult).then_inc(y_ready, 1)
            dve.wait_ge(base_ready, 1)
            dve.wait_ge(fan_done, 1)
            step(nc.vector.tensor_tensor(h[:].rearrange("p b c -> p (b c)").rearrange("p (k n) -> p k n", k=2),
                                         base[:].rearrange("p b c -> p (b c)").rearrange("p (k n) -> p k n", k=2),
                                         ps[:, 0:2, :], ALU.add))
            step(nc.vector.tensor_reduce(small[:, 0, :], h[:], AX.X, ALU.add))
            step(nc.vector.tensor_scalar(small[:, 4, :], small[:, 0, :], 1.0 / C, None, ALU.mult))
            nc.vector.tensor_tensor(tmp[:], h[:], over_c(small[:, 4, :]), ALU.subtract).then_inc(act_in, 1)
            dve.wait_ge(act_out, 7)
            step(nc.vector.tensor_reduce(small[:, 0, :], tmp2[:], AX.X, ALU.add))
            root(small[:, 0, :], 1.0 / C, LN_EPS, 8)
            nc.vector.tensor_tensor(tmp[:], tmp[:], over_c(small[:, 5, :]), ALU.mult).then_inc(x2_ready, 1)

            def over_e(ap):
                return ap.unsqueeze(2).to_broadcast([P, NB, NE])

            dve.wait_ge(logit_psum, 1)
            step(nc.vector.tensor_tensor(rt[:, 4], ps[:, 6, 0:NB * NE].rearrange("p (b e) -> p b e", e=NE),
                                         rw("rb2").unsqueeze(1).to_broadcast([P, NB, NE]), ALU.add))
            step(nc.vector.tensor_reduce(small[:, 6, :], rt[:, 4], AX.X, ALU.max))
            nc.vector.tensor_tensor(rt[:, 0], rt[:, 4], over_e(small[:, 6, :]), ALU.subtract).then_inc(act_in, 1)
            dve.wait_ge(act_out, 9)
            step(nc.vector.tensor_reduce(small[:, 6, :], rt[:, 1], AX.X, ALU.add))
            step(nc.vector.reciprocal(small[:, 7, :], small[:, 6, :]))
            nc.vector.tensor_tensor(rt[:, 2], rt[:, 1], over_e(small[:, 7, :]), ALU.mult).then_inc(act_in, 1)
            dve.wait_ge(act_in, 9)
            mine = rt[:, 2].unsqueeze(3).to_broadcast([P, NB, NE, NE])
            other = rt[:, 2].unsqueeze(2).to_broadcast([P, NB, NE, NE])
            lower = rw("lower").rearrange("p (e f) -> p e f", e=NE).unsqueeze(1).to_broadcast([P, NB, NE, NE])
            step(nc.vector.tensor_tensor(rank6[:, 0], other, mine, ALU.is_equal))
            step(nc.vector.tensor_tensor(rank6[:, 0], rank6[:, 0], lower, ALU.mult))
            step(nc.vector.tensor_tensor(rank6[:, 1], other, mine, ALU.is_gt))
            step(nc.vector.tensor_tensor(rank6[:, 0], rank6[:, 0], rank6[:, 1], ALU.add))
            step(nc.vector.tensor_reduce(rt[:, 5], rank6[:, 0], AX.X, ALU.add))
            step(nc.vector.tensor_scalar(rt[:, 6], rt[:, 5], 1.5, None, ALU.is_lt))
            dve.wait_ge(act_out, 10)
            step(nc.vector.tensor_tensor(rt[:, 6], rt[:, 6], rt[:, 3], ALU.mult))
            step(nc.vector.tensor_reduce(small[:, 6, :], rt[:, 6], AX.X, ALU.add))
            step(nc.vector.reciprocal(small[:, 7, :], small[:, 6, :]))
            nc.vector.tensor_tensor(rt[:, 7], rt[:, 6], over_e(small[:, 7, :]), ALU.mult).then_inc(cw_ready, 1)

            def finish_chunk(n):
                i, g = CHUNKS[n]
                dve.wait_ge(y_psum, NP * (n + 1))
                where = slice(g, g + CHUNK_B)
                nc.vector.tensor_tensor(
                    result.rearrange("p (g i) c -> p i g c", i=2)[:, i, where, :],
                    h[:].rearrange("p (g i) c -> p i g c", i=2)[:, i, where, :],
                    ps[:, 6 + n % 2, 0:CHUNK_B * C].rearrange("p (g c) -> p g c", g=CHUNK_B),
                    ALU.add).then_inc(result_ready, 1)

            for u, (n, p) in enumerate(UNITS):
                dve.wait_ge(h2_ready, u + 1)
                if u >= 2:
                    dve.wait_ge(y_psum, u - 1)
                nc.vector.tensor_tensor(H2c[:, u % 2, :], H2[:, u % 2, :], ps[:, 4 + u % 2, :],
                                        ALU.mult).then_inc(h2c_ready, 1)
                if p == 0 and n >= 1:
                    finish_chunk(n - 1)
            finish_chunk(len(CHUNKS) - 1)

        @block.tensor
        def _(pe):
            pe.sem_inc(half_free, 2)
            pe.sem_inc(vp_ready, BG)

            pe.wait_ge(pool_step, 1)
            for k in range(2):
                pe.wait_ge(stat_ready, k + 1)
                nc.tensor.matmul(ps[:, 0, k * NB:(k + 1) * NB], ones[:], small[:, 0, :], start=(k == 0), stop=True,
                                 skip_group_check=True).then_inc(stat_summed, 1)
            pe.wait_ge(xn_ready, 1)
            for b in range(NB):
                ins = nc.tensor.transpose(ps[:, b // 4, (b % 4) * T:(b % 4 + 1) * T],
                                          xn2x[:, b, :, :].rearrange("p i c -> p (i c)"), ident)
                if b % 4 == 3:
                    ins.then_inc(xt_psum, 1)
            pe.wait_ge(xt_ready, 4)
            for b in range(NB):
                ins = nc.tensor.matmul(ps[:, 4, b * NH:(b + 1) * NH], XT[0:C, b, :], wk8[0:C, :],
                                       start=(b == 0), stop=True, skip_group_check=True)
            ins.then_inc(xw_psum, 1)

            def project_q(x):
                for turn in range(2):
                    for k in range(2):
                        for half in range(2):
                            rows = slice(C * half, C * half + C)
                            ins = nc.tensor.matmul(ps[:, 4 + 2 * turn + half, k * GC:(k + 1) * GC],
                                                   wq[rows, 2 * turn + k, :],
                                                   x[rows, :, :],
                                                   start=(k == 0), stop=True, skip_group_check=True)
                    ins.then_inc(qp_ready, 1)

            def start_distances(G):
                pe.wait_ge(q_ready, G * 2 + 2)
                for hd in range(NH):
                    nc.tensor.matmul(R[:, hd, :], start_w[:, hd, :], qn[:, hd, :, :],
                                     start=(hd % HEADS_PER_BANK == 0), stop=False, skip_group_check=True)

            def group(G, last):
                with pe.Fori(0, NJ // 2) as J:
                    for half in range(2):
                        pe.wait_ge(win_ready, G * NHALF + J * 2 + (half + 1))
                        pe.wait_ge(dve_half, G * NHALF + J * 2 + (half + 1))
                        pe.wait_ge(act_half, G * NHALF + J * 2 + (half + 1))
                        for hd in range(NH):
                            for g in range(TQ):
                                ins = nc.tensor.matmul(R[32 * g:32 * g + 32, hd, :], window[:, half, hd, :],
                                                       D[:, half, g, hd * GC:(hd + 1) * GC],
                                                       start=False, stop=False, skip_group_check=True,
                                                       tile_position=(0, 32 * g))
                        ins.then_inc(half_free, 1)
                pe.wait_ge(x_copied, G + 1)
                if not last:
                    project_q(x_next)
                for b in range(BG):
                    if last:
                        pe.wait_ge(q_ready, G * 2 + 2)
                    else:
                        pe.wait_ge(q_ready, G * 2 + (3 + b))
                    for half in range(2):
                        rows = slice(C * half, C * half + C)
                        ins = nc.tensor.matmul(ps[:, 4 + 2 * b + half, :], x_now[rows, b, :], wv[rows, :],
                                               start=True, stop=True)
                    ins.then_inc(vp_ready, 1)
                if not last:
                    pe.wait_ge(e_ready, G * BANKS + BANKS)
                    start_distances(G + 1)
                pe.wait_ge(v_ready, G * BG + BG)
                for k in range(BANKS):
                    pe.wait_ge(a_ready, G * BANKS + (k + 1))
                    if k >= 2:
                        pe.wait_ge(at_ready, G * BANKS + (k - 1))
                    for n in range(HEADS_PER_BANK * BG):
                        ins = nc.tensor.transpose(ps[:, 4 + k % 2, n * T:(n + 1) * T],
                                                  A[:, 2 * k + n // 2, n % 2, :], ident)
                    ins.then_inc(tp_ready, 1)
                for k in range(BANKS):
                    pe.wait_ge(at_ready, G * BANKS + (k + 1))
                    for hd in range(HEADS_PER_BANK * k, HEADS_PER_BANK * (k + 1)):
                        for d in range(2):
                            for b in range(BG):
                                attn = (AT, A)[d]
                                ins = nc.tensor.matmul(ps[C * b:C * b + C, 6, 0:T],
                                                       V[:, b, d, hd * C:(hd + 1) * C], attn[:, hd, b, :],
                                                       start=(hd == 0 and d == 0), stop=(hd == NH - 1 and d == 1),
                                                       skip_group_check=True)
                ins.then_inc(o_done, 1)
                if not last:
                    pe.wait_ge(o_saved, G + 1)

            pe.wait_ge(xw_ready, 1)
            project_q(XT[:, 0:BG, :])
            pe.wait_ge(pool_step, 5)
            start_distances(0)
            with pe.Fori(0, NG - 1) as G:
                group(G, False)
            group(NG - 1, True)

            pe.wait_ge(y_ready, 1)
            for g in range(NG):
                ins = nc.tensor.matmul(ps[:, g // 4, (g % 4) * P:(g % 4 + 1) * P], yT[:, g, :], cst("fan"),
                                       start=(g % 4 == 0), stop=True, skip_group_check=True)
            ins.then_inc(fan_done, 1)
            pe.wait_ge(x2_ready, 1)
            for g in range(NG):
                ins = nc.tensor.transpose(ps[:, g // 4, (g % 4) * P:(g % 4 + 1) * P],
                                          tmp[:, BG * g:BG * g + BG, :].rearrange("p b c -> p (b c)"), ident)
                if g % 4 == 3:
                    ins.then_inc(x2t_psum, 1)
            for n, (i, g) in enumerate(CHUNKS):
                pe.wait_ge(x2t_ready, g // 4 + 1)
                half = slice(C * i, C * i + C)
                nc.tensor.matmul(ps[0:RH, 2 + n, :], cst("rw1")[half, :], X2T[half, g:g + CHUNK_B, :],
                                 start=True, stop=True).then_inc(rh_psum, 1)
            for b in range(NB):
                g, i = b // 2, b % 2
                pe.wait_ge(rh_ready, (g // 4) * 2 + i + 1)
                ins = nc.tensor.matmul(ps[:, 6, b * NE:(b + 1) * NE], rhT[0:RH, i, g, :], cst("rw2")[0:RH, :],
                                       start=(b == 0), stop=True, skip_group_check=True)
            ins.then_inc(logit_psum, 1)
            pe.wait_ge(cw_ready, 1)
            for i in range(2):
                for g in range(NG):
                    n = i * NG + g
                    ins = nc.tensor.transpose(ps[0:NE, n // 4, (n % 4) * T:(n % 4 + 1) * T], rt[:, 7, 2 * g + i, :], ident)
                    if n % 4 == 3:
                        ins.then_inc(cwt_psum, 1)
            pe.wait_ge(cwt_ready, 4)

            def first_layer(u):
                n, p = UNITS[u]
                i, g = CHUNKS[n]
                half = slice(C * i, C * i + C)
                if u >= 2:
                    pe.wait_ge(h1_ready, u - 1)
                nc.tensor.matmul(ps[:, u % 2, :], cst("w1")[half, p * P:(p + 1) * P], X2T[half, g:g + CHUNK_B, :],
                                 start=True, stop=True).then_inc(h1_psum, 1)

            def second_layer(u):
                n, p = UNITS[u]
                i, g = CHUNKS[n]
                if u >= 2:
                    pe.wait_ge(h2c_ready, u - 1)
                nc.tensor.matmul(ps[:, 4 + u % 2, :], cst("pick")[0:NE, p * P:(p + 1) * P],
                                 cwT[0:NE, i, g:g + CHUNK_B, :], start=True, stop=True)
                pe.wait_ge(h1_ready, u + 1)
                nc.tensor.matmul(ps[:, 2 + u % 2, :], cst("w2")[:, p * P:(p + 1) * P], H1[:, u % 2, :],
                                 start=True, stop=True).then_inc(h2_psum, 1)

            def third_layer(u):
                n, p = UNITS[u]
                i, g = CHUNKS[n]
                if p == 0 and n >= 2:
                    pe.wait_ge(result_ready, n - 1)
                if p == 0:
                    for k in range(CHUNK_B):
                        nc.tensor.matmul(ps[:, 6 + n % 2, k * C:(k + 1) * C], cwT[0:NE, i, g + k, :],
                                         cst("b3")[0:NE, :], start=(k == 0), stop=False, skip_group_check=True)
                pe.wait_ge(h2c_ready, u + 1)
                for k in range(CHUNK_B):
                    ins = nc.tensor.matmul(ps[:, 6 + n % 2, k * C:(k + 1) * C], H2c[:, u % 2, k * T:(k + 1) * T],
                                           cst("w3")[:, p * C:(p + 1) * C], start=False, stop=(p == NP - 1),
                                           skip_group_check=True)
                ins.then_inc(y_psum, 1)

            for u in range(len(UNITS) + 2):
                if u < len(UNITS):
                    first_layer(u)
                if 1 <= u <= len(UNITS):
                    second_layer(u - 1)
                if u >= 2:
                    third_layer(u - 2)


def _pack(inputs):
    import numpy as np

    g = {k: np.asarray(v) for k, v in inputs.items()}
    dt = g["x"].dtype
    x_pad = np.zeros((NB, T_IN + 4, C), dt)
    x_pad[:, 1:T_IN + 1] = g["x"]

    wqv_t = g["L0_attn_wqv_w"].T
    cols = np.zeros((P, NCOLS), dt)

    def put(name, rows, value):
        a, b = COLS[name]
        cols[rows, a:b] = value.reshape(value.shape[0], -1)

    put("ident", slice(0, P), np.eye(P, dtype=dt))
    q_t = wqv_t[:, :NH * C].reshape(C, NH, 1, C)
    q_t = np.concatenate([q_t, q_t], axis=2)
    v_t = wqv_t[:, NH * C:]
    bq = g["L0_attn_wqv_b"][:NH * C].reshape(NH, C).T
    fan_t = g["L0_attn_fanin_w"].T
    w1 = g["L0_ffn_expert_w1"].transpose(1, 0, 2)
    for i in range(2):
        rows = slice(C * i, C * i + C)
        put("wq", rows, q_t[:, 4 * i:4 * i + 4])
        put("wv", rows, v_t[:, NH * C * i:NH * C * (i + 1)])
        put("wk", rows, g["L0_attn_wk"].T)
        put("bq", rows, bq)
        put("w1", rows, w1)
        put("rw1", rows, g["L0_ffn_router_w1"])
        put("w3", rows, g["L0_ffn_expert_w3"][i::2].transpose(1, 0, 2))
        put("b1", rows, g["L0_ffn_expert_b1"][i::2].T)
        put("b2", rows, g["L0_ffn_expert_b2"][i::2].T)
        a = COLS["fan"][0] + C * i
        cols[rows, a:a + C] = fan_t
        for p in range(NP):
            a = COLS["w2"][0] + p * P + C * i
            cols[rows, a:a + C] = g["L0_ffn_expert_w2"][2 * p + i]
            a = COLS["pick"][0] + p * P + C * i
            cols[2 * p + i, a:a + C] = 1
    put("rw2", slice(0, RH), g["L0_ffn_router_w2"])
    put("rb1", slice(0, RH), g["L0_ffn_router_b1"].reshape(RH, 1))
    put("b3", slice(0, NE), g["L0_ffn_expert_b3"])

    lower = np.tril(np.ones((NE, NE), dt), -1)
    parts = {"conv_w": g["L0_tok_w"], "conv_b": g["L0_tok_b"], "gamma": g["L0_tok_gamma"], "beta": g["L0_tok_beta"],
             "alpha": g["L0_tok_alpha"], "fan_b": g["L0_attn_fanin_b"], "bv": g["L0_attn_wqv_b"][NH * C:],
             "rb2": g["L0_ffn_router_b2"], "lower": lower}
    rows = np.concatenate([parts[name].reshape(-1) for name in ROWS]).reshape(NROWS)
    return {"x_pad": x_pad, "cols": cols, "rows": rows}


def kernel(**inputs):
    import concourse.bacc as _bacc
    from concourse.bass_utils import run_bass_kernel_spmd as _run

    arrays = _pack(inputs)
    nc = _bacc.Bacc("TRN2", target_bir_lowering=False, num_devices=1)
    args = [nc.dram_tensor(name, a.shape, mybir.dt.from_np(a.dtype), kind="ExternalInput").ap()
            for name, a in arrays.items()]
    out = nc.dram_tensor("out", (NB, T, C), F32, kind="ExternalOutput").ap()
    build(nc, *args, out)
    return _run(nc, [arrays], core_ids=[0]).results[0]["out"]
```

```python
from contextlib import ExitStack

import concourse.bass as bass
from concourse import mybir

F32 = mybir.dt.float32
BF16 = mybir.dt.bfloat16
ALU = mybir.AluOpType
ACT = mybir.ActivationFunctionType
AX = mybir.AxisListType

NB, T_IN, C = 16, 256, 64
TAPS = 5
T = T_IN // 2
NH = 8
P = 128
BG = 2
NG = NB // BG
GC = BG * T
TQ = 4
NJ = 32 // 2
HEADS_PER_BANK = 512 // GC
NE, RH = 6, 32
TINY = 1e-30
CONV_EPS, LN_EPS = 1e-3, 1e-5
X_ROWS = T_IN + 4
LOAD_G = 2
GH = NG // 2
PARTS = 3
CK = PARTS * BG * NE

COLS = {}
for _names in ([("ident", P), ("conv_w", TAPS), ("wk", NH), ("bq", NH), ("wq", 4 * 2 * C), ("wv", NH * C)],
               [("fan", P), ("rw1", BG * RH), ("rw2", BG * NE), ("rb1", 1), ("b1", NE), ("b2", NE), ("b3", P),
                ("w1", NE * P), ("w2", NE * P), ("w3", NE * P), ("pick", NE * P)]):
    _at = 0
    for _name, _n in _names:
        COLS[_name] = (len(_names) > 6, _at, _at + _n)
        _at += _n
    if len(_names) > 6:
        NCOLS2 = _at
    else:
        NCOLS = _at
ROWS = {}
_at = 0
for _name, _n in [("conv_b", 2 * C), ("gamma", C), ("beta", C), ("alpha", C), ("fan_b", C),
                  ("bv", 2 * NH * C), ("rb2", NE), ("lower", NE * NE)]:
    ROWS[_name] = (_at, _at + _n)
    _at += _n
NROWS = _at


def build(nc, x_t, cols, cols2, rows, out):
    with ExitStack() as ctx:
        def sb(name, shape):
            return ctx.enter_context(nc.sbuf_tensor(name, shape, F32))

        def sem(name):
            return ctx.enter_context(nc.semaphore(name))

        const = [sb("const", [P, NCOLS]), sb("const2", [P, NCOLS2])]
        row = sb("row", [P, NROWS])
        xc = sb("xc", [P, NG, X_ROWS])
        conv = sb("conv", [P, TAPS, P])
        pick_b = ctx.enter_context(nc.sbuf_tensor("pick_b", [P, NE * P], BF16))
        part_b = ctx.enter_context(nc.sbuf_tensor("part_b", [P, NB * NE], BF16))
        cwT_b = ctx.enter_context(nc.sbuf_tensor("cwT_b", [P, NG, T], BF16))
        h = sb("h", [P, NB, C])
        base = sb("base", [P, NB, C])
        xn2x = sb("xn2x", [P, NB, 2, C])
        tmp = sb("tmp", [P, NB, C])
        tmp2 = sb("tmp2", [P, NB, C])
        small = sb("small", [P, 8, NB])
        ones = sb("ones", [P, P])
        XT = sb("XT", [P, NB, T])
        x_now = sb("x_now", [P, BG, T])
        x_next = sb("x_next", [P, BG, T])
        neg_x = sb("neg_x", [P, NB, NJ, TQ])
        neg_xw = sb("neg_xw", [P, NB, NH])
        abs_wk = sb("abs_wk", [P, NH])
        sgn_wk = sb("sgn_wk", [P, NH])
        inv_wk = sb("inv_wk", [P, NH])
        wk8 = sb("wk8", [P, NH])
        start_w = sb("start_w", [P, NH, P])
        hot = sb("hot", [P, NH, 62])
        window = sb("window", [P, 2, NH, 32])
        qn = sb("qn", [P, NH, BG, T])
        D = sb("D", [P, 2, TQ, NH * GC])
        V = sb("V", [P, BG, 2, NH * C])
        A = sb("A", [P, NH, BG, T])
        AT = sb("AT", [P, NH, BG, T])
        den = sb("den", [P, NH, BG])
        den1 = sb("den1", [P, NH, BG])
        rden = sb("rden", [P, NH, BG])
        OT = sb("OT", [P, NG, T])
        ps = ctx.enter_context(nc.psum_tensor("ps", [P, 8, 512], F32))
        R = ps[:, 0:4, :].rearrange("p k (h n) -> p (k h) n", n=GC)

        def cst(name):
            k, a, b = COLS[name]
            return const[k][:, a:b]

        def rw(name):
            a, b = ROWS[name]
            return row[:, a:b]

        ident = cst("ident")
        wq = cst("wq").rearrange("p (m n) -> p m n", m=4)
        wv = cst("wv")
        Dt = D[:, 0, :, :].rearrange("p g n -> p (g n)")
        Du = D[:, 1, :, :].rearrange("p g n -> p (g n)")
        gate = Dt[:, 0:1024].rearrange("p (g t) -> p g t", g=NG)
        yT = Dt[:, 1024:2048].rearrange("p (g t) -> p g t", g=NG)
        X2T = Dt[:, 2048:3072].rearrange("p (g t) -> p g t", g=NG)
        rhT = Dt[:, 3072:4096].rearrange("p (g t) -> p g t", g=NG)
        cwT = Dt[:, 4096:5120].rearrange("p (g t) -> p g t", g=NG)
        cw = Dt[:, 5120:5120 + NG * CK].rearrange("p (g k n) -> p g k n", g=NG, k=PARTS)
        H1 = Du[:, 0:1024].rearrange("p (k n) -> p k n", k=2)
        H2 = Du[:, 1024:2048].rearrange("p (k n) -> p k n", k=2)
        H2c = Du[:, 2048:3072].rearrange("p (k n) -> p k n", k=2)
        result = Du[:, 3072:4096].rearrange("p (b c) -> p b c", b=NB)
        rt = Du[:, 4096:4096 + 8 * 96].rearrange("p (k b e) -> p k b e", k=8, e=NE)
        rank6 = Du[:, 5120:5120 + 2 * 576].rearrange("p (k b e f) -> p k b e f", k=2, b=NB, e=NE)

        const_loaded, const2_loaded, rows_loaded = sem("const_loaded"), sem("const2_loaded"), sem("rows_loaded")
        x_loaded = [sem(f"x_loaded{i}") for i in range(NG // LOAD_G)]
        dve_step = sem("dve_step")
        pool_step = sem("pool_step")
        wk_ready = sem("wk_ready")
        conv_ready, conv_done = sem("conv_ready"), sem("conv_done")
        stat_ready, stat_summed = sem("stat_ready"), sem("stat_summed")
        act_in, act_out = sem("act_in"), sem("act_out")
        xn_ready, xt_psum, xt_ready = sem("xn_ready"), sem("xt_psum"), sem("xt_ready")
        neg_x_ready = sem("neg_x_ready")
        xw_psum, xw_ready = sem("xw_psum"), sem("xw_ready")
        base_ready = sem("base_ready")
        x_copied = sem("x_copied")
        qp_ready = sem("qp_ready")
        q_ready = sem("q_ready")
        vp_ready, v_ready = sem("vp_ready"), sem("v_ready")
        win_ready = sem("win_ready")
        dve_half, act_half = sem("dve_half"), sem("act_half")
        half_free = sem("half_free")
        e_ready = sem("e_ready")
        norm_step = sem("norm_step")
        a_ready = sem("a_ready")
        tp_ready, at_ready = sem("tp_ready"), sem("at_ready")
        o_done, o_saved = sem("o_done"), sem("o_saved")
        gate_ready, centred, squared = sem("gate_ready"), sem("centred"), sem("squared")
        y_ready, fan_done = sem("y_ready"), sem("fan_done")
        x2_ready, x2t_psum, x2t_ready = sem("x2_ready"), sem("x2t_psum"), sem("x2t_ready")
        rh_psum, rh_ready, logit_psum = sem("rh_psum"), sem("rh_ready"), sem("logit_psum")
        pick_ready = sem("pick_ready")
        cw_ready, cwt_psum, cwt_ready = sem("cw_ready"), sem("cwt_psum"), sem("cwt_ready")
        h1_psum, h1_ready = sem("h1_psum"), sem("h1_ready")
        h2_psum, h2_ready = sem("h2_psum"), sem("h2_ready")
        h2c_ready = sem("h2c_ready")
        y_psum, result_ready, stored = sem("y_psum"), sem("result_ready"), sem("stored")

        NHALF = 2 * NJ // 2
        BANKS = 4
        ACT_PIECES = ((0, 1), (2, 1), (3, 1))
        UNITS = [(n, e) for n in range(2) for e in range(NE)]

        def bs(n):
            return slice(n * NB // 2, (n + 1) * NB // 2)

        block = ctx.enter_context(nc.Block())

        @block.sync
        def _(sp):
            for k in range(NG // LOAD_G):
                g = slice(k * LOAD_G, (k + 1) * LOAD_G)
                sp.dma_start(xc[:, g, :], x_t[:, g, :]).then_inc(x_loaded[k], 16)
            sp.dma_start(const[1][:], cols2).then_inc(const2_loaded, 16)
            for n in range(2):
                sp.wait_ge(result_ready, n + 1)
                b = slice(n * NB // 2, (n + 1) * NB // 2)
                sp.dma_start(out[b].rearrange("b t c -> t b c"), result[:, b, :]).then_inc(stored, 16)
            sp.wait_ge(stored, 32)

        @block.gpsimd
        def _(pool):
            steps = [0]

            def step(ins):
                steps[0] += 1
                ins.then_inc(pool_step, 1)
                pool.wait_ge(pool_step, steps[0])

            step(nc.gpsimd.memset(ones[:], 1.0))
            step(nc.gpsimd.memset(hot[:], 0.0))
            pool.wait_ge(wk_ready, 1)
            step(nc.gpsimd.tensor_copy(hot[0:C, :, 30], abs_wk[0:C, :]))
            step(nc.gpsimd.tensor_copy(hot[C:P, :, 31], abs_wk[C:P, :]))
            step(nc.gpsimd.tensor_scalar(start_w[:], abs_wk[:].unsqueeze(2).to_broadcast([P, NH, P]), -0.25, None,
                                         ALU.mult))
            pool.wait_ge(xn_ready, 4)
            step(nc.gpsimd.tensor_tensor(base[:], h[:], xn2x[:, :, 0, :], ALU.add))
            nc.gpsimd.tensor_tensor(base[:], base[:], rw("fan_b").unsqueeze(1).to_broadcast([P, NB, C]),
                                    ALU.add).then_inc(base_ready, 1)

            def group(G, last):
                pool.wait_ge(vp_ready, G * BG + BG)
                flat = XT[:].rearrange("p b t -> p (b t)")
                copy = nc.gpsimd.tensor_copy(x_now[:].rearrange("p b t -> p (b t)"), flat[:, bass.ds(G * GC, GC)])
                if not last:
                    copy = nc.gpsimd.tensor_copy(x_next[:].rearrange("p b t -> p (b t)"),
                                                 flat[:, bass.ds(G * GC + GC, GC)])
                copy.then_inc(x_copied, 1)
                with pool.Fori(0, NJ // 2) as J:
                    for half in range(2):
                        pool.wait_ge(half_free, G * NHALF + J * 2 + (half + 1))
                        nc.gpsimd.tensor_copy(window[:, half, :, :],
                                              hot[:, :, bass.ds(J * -4 + (30 - 2 * half), 32)]).then_inc(win_ready, 1)

            pool.wait_ge(xt_ready, 4)
            with pool.Fori(0, NG - 1) as G:
                group(G, False)
            group(NG - 1, True)
            pool.wait_ge(const2_loaded, 16)
            nc.gpsimd.tensor_copy(pick_b[:], cst("pick")).then_inc(pick_ready, 1)

        def relu_piece(engine, G, J, half, g, b):
            dst = D[:, half, g, :].rearrange("p (h b t) -> p h b t", h=NH, b=BG)[:, :, b, :]
            minus_x = neg_x[:].rearrange("p b j g -> p (b j g)")[
                :, bass.ds(G * (BG * NJ * TQ) + J * (2 * TQ) + (b * NJ * TQ + half * TQ + g), 1)]
            if engine is nc.scalar:
                return nc.scalar.activation(dst, qn[:, :, b, :], ACT.Relu, bias=minus_x)
            return nc.vector.tensor_scalar(dst, qn[:, :, b, :], minus_x, 0.0, ALU.add, ALU.max)

        PIECES = [(g, b) for g in range(TQ) for b in range(BG)]

        @block.scalar
        def _(act):
            act.dma_start(const[0][:], cols).then_inc(const_loaded, 16)
            act.dma_start(row[:], rows.partition_broadcast(P)).then_inc(rows_loaded, 16)

            act.wait_ge(act_in, 1)
            nc.scalar.activation(tmp2[:], tmp[:], ACT.Square).then_inc(act_out, 1)
            act.wait_ge(act_in, 2)
            nc.scalar.activation(small[:, 2, :], small[:, 1, :], ACT.Sqrt).then_inc(act_out, 1)
            act.wait_ge(act_in, 3)
            nc.scalar.activation(tmp2[:], tmp[:], ACT.Relu).then_inc(act_out, 1)
            act.wait_ge(act_in, 4)
            nc.scalar.activation(tmp2[:], tmp[:], ACT.Square).then_inc(act_out, 1)
            act.wait_ge(act_in, 5)
            nc.scalar.activation(small[:, 2, :], small[:, 1, :], ACT.Sqrt).then_inc(act_out, 1)
            for k in range(4):
                act.wait_ge(xt_psum, k + 1)
                nc.scalar.activation(XT[:, 4 * k:4 * k + 4, :],
                                     ps[:, k, :].rearrange("p (b t) -> p b t", b=4), ACT.Copy).then_inc(xt_ready, 1)

            def group(G, last):
                act.wait_ge(q_ready, G * 2 + 2)
                with act.Fori(0, NJ // 2) as J:
                    for half in range(2):
                        act.wait_ge(half_free, G * NHALF + J * 2 + (half + 1))
                        for g, b in ACT_PIECES:
                            piece = relu_piece(nc.scalar, G, J, half, g, b)
                        piece.then_inc(act_half, 1)
                act.wait_ge(half_free, G * NHALF + (NHALF + 2))
                for k in range(BANKS):
                    for hd in range(HEADS_PER_BANK * k, HEADS_PER_BANK * (k + 1)):
                        for b in range(BG):
                            e = nc.scalar.activation(
                                A[:, hd, b, :], R[:, hd, b * T:(b + 1) * T], ACT.Exp, scale=-0.25,
                                bias=neg_xw[:].rearrange("p b h -> p (b h)")[:, bass.ds(G * (BG * NH) + (b * NH + hd), 1)],
                                accum_out=den[:, hd, b:b + 1])
                    e.then_inc(e_ready, 1)
                for k in range(BANKS):
                    act.wait_ge(tp_ready, G * BANKS + (k + 1))
                    nc.scalar.activation(AT[:, 2 * k:2 * k + 2, :, :],
                                         ps[:, 4 + k % 2, :].rearrange("p (h b t) -> p h b t", h=2, b=BG),
                                         ACT.Copy).then_inc(at_ready, 1)

            act.wait_ge(xw_ready, 1)
            nc.scalar.activation(small[:, 7, :], small[:, 5, :], ACT.Exp, scale=0.0)
            act.wait_ge(neg_x_ready, 8)
            with act.Fori(0, NG - 1) as G:
                group(G, False)
            group(NG - 1, True)

            act.wait_ge(o_saved, NG)
            for n in range(2):
                gs = slice(n * GH, (n + 1) * GH)
                nc.scalar.activation(gate[:, gs, :], OT[:, gs, :], ACT.Sigmoid, scale=1.702).then_inc(gate_ready, 1)
            for n in range(2):
                act.wait_ge(centred, n + 1)
                nc.scalar.activation(tmp2[:, bs(n), :], tmp[:, bs(n), :], ACT.Square).then_inc(squared, 1)
            act.wait_ge(act_in, 6)
            nc.scalar.activation(small[:, 2, :], small[:, 1, :], ACT.Sqrt).then_inc(act_out, 1)
            act.wait_ge(act_in, 6)
            nc.scalar.activation(small[:, 7, :], small[:, 1, :], ACT.Exp, scale=0.0)
            for n in range(2):
                act.wait_ge(x2t_psum, n + 1)
                nc.scalar.activation(X2T[:, n * GH:(n + 1) * GH, :],
                                     ps[:, 2 + n, :].rearrange("p (g t) -> p g t", g=GH), ACT.Copy).then_inc(x2t_ready, 1)
            for n in range(2):
                act.wait_ge(rh_psum, n + 1)
                nc.scalar.activation(rhT[0:BG * RH, n * GH:(n + 1) * GH, :],
                                     ps[0:BG * RH, 4 + n, :].rearrange("p (g t) -> p g t", g=GH),
                                     ACT.Relu, bias=cst("rb1")[0:BG * RH, :]).then_inc(rh_ready, 1)
            act.wait_ge(act_in, 7)
            nc.scalar.activation(rt[:, 1], rt[:, 0], ACT.Exp).then_inc(act_out, 1)
            act.wait_ge(act_in, 8)
            nc.scalar.activation(rt[:, 3], rt[:, 2], ACT.Exp).then_inc(act_out, 1)
            for u, (n, e) in enumerate(UNITS):
                act.wait_ge(h1_psum, u + 1)
                if u >= 2:
                    act.wait_ge(h2_psum, u - 1)
                nc.scalar.activation(H1[:, u % 2, :], ps[:, u % 2, :], ACT.Relu,
                                     bias=cst("b1")[:, e:e + 1]).then_inc(h1_ready, 1)
                if u == 0:
                    for m in range(2):
                        gs = slice(m * GH, (m + 1) * GH)
                        act.wait_ge(cwt_psum, m + 1)
                        src = ps[0:CK, 6 + m, :].rearrange("p (g t) -> p g t", g=GH)
                        nc.scalar.activation(cwT_b[0:CK, gs, :], src, ACT.Copy).then_inc(cwt_ready, 1)
                        nc.scalar.activation(cwT[0:CK, gs, :], src, ACT.Copy).then_inc(cwt_ready, 1)
                act.wait_ge(h2_psum, u + 1)
                if u >= 2:
                    act.wait_ge(h2c_ready, u - 1)
                nc.scalar.activation(H2[:, u % 2, :], ps[:, 2 + u % 2, :], ACT.Relu,
                                     bias=cst("b2")[:, e:e + 1]).then_inc(h2_ready, 1)

        @block.vector
        def _(dve):
            steps = [0]

            def step(ins):
                steps[0] += 1
                ins.then_inc(dve_step, 1)
                dve.wait_ge(dve_step, steps[0])

            def over_c(ap):
                return ap.unsqueeze(2).to_broadcast([P, NB, C])

            def over_b(ap):
                return ap.unsqueeze(1).to_broadcast([P, NB, C])

            dve.wait_ge(const_loaded, 16)
            step(nc.vector.tensor_scalar(inv_wk[:], cst("wk"), -1.0, None, ALU.mult))
            step(nc.vector.tensor_tensor(abs_wk[:], cst("wk"), inv_wk[:], ALU.max))
            step(nc.vector.tensor_scalar(abs_wk[:], abs_wk[:], TINY, None, ALU.max))
            step(nc.vector.tensor_scalar(sgn_wk[:], cst("wk"), 0.0, 2.0, ALU.is_ge, ALU.mult))
            step(nc.vector.tensor_scalar(sgn_wk[:], sgn_wk[:], -1.0, None, ALU.add))
            step(nc.vector.reciprocal(inv_wk[:], abs_wk[:]))
            step(nc.vector.tensor_tensor(inv_wk[:], inv_wk[:], sgn_wk[:], ALU.mult))
            nc.vector.tensor_scalar(wk8[:], abs_wk[:], -0.125, None, ALU.mult).then_inc(wk_ready, 1)

            for k in range(TAPS):
                ins = nc.vector.tensor_scalar(conv[:, k, :], ident, cst("conv_w")[:, k:k + 1], None, ALU.mult)
            ins.then_inc(conv_ready, 1)

            y = ps[:, 0:2, :].rearrange("p k n -> p (k n)").rearrange("p (b c) -> p b c", b=NB)
            for k in range(2):
                dve.wait_ge(conv_done, k + 1)
                red = nc.vector.tensor_reduce(small[:, 0, bs(k)], y[:, bs(k), :], AX.X, ALU.add)
            red.then_inc(stat_ready, 1)
            dve.wait_ge(stat_summed, 1)
            step(nc.vector.tensor_scalar(small[:, 3, :], ps[:, 2, 0:NB], 1.0 / (T * C), None, ALU.mult))
            nc.vector.tensor_tensor(tmp[:], y, over_c(small[:, 3, :]), ALU.subtract).then_inc(act_in, 1)
            dve.wait_ge(act_out, 1)
            nc.vector.tensor_reduce(small[:, 0, :], tmp2[:], AX.X, ALU.add).then_inc(stat_ready, 1)
            dve.wait_ge(rows_loaded, 16)
            dve.wait_ge(stat_summed, 2)

            def root(source, scale, eps, turn):
                nc.vector.tensor_scalar(small[:, 1, :], source, scale, eps, ALU.mult, ALU.add).then_inc(act_in, 1)
                dve.wait_ge(act_out, turn)
                step(nc.vector.reciprocal(small[:, 3, :], small[:, 2, :]))
                step(nc.vector.tensor_tensor(small[:, 3, :], small[:, 3, :], small[:, 1, :], ALU.mult))
                step(nc.vector.tensor_tensor(small[:, 3, :], small[:, 3, :], small[:, 2, :], ALU.add))
                step(nc.vector.tensor_scalar(small[:, 3, :], small[:, 3, :], 0.5, None, ALU.mult))
                step(nc.vector.reciprocal(small[:, 5, :], small[:, 3, :]))

            root(ps[:, 2, NB:2 * NB], 1.0 / (T * C), CONV_EPS, 2)
            step(nc.vector.tensor_tensor(h[:], over_b(rw("gamma")), over_c(small[:, 5, :]), ALU.mult))
            step(nc.vector.tensor_tensor(tmp[:], tmp[:], h[:], ALU.mult))
            nc.vector.tensor_tensor(tmp[:], tmp[:], over_b(rw("beta")), ALU.add).then_inc(act_in, 1)
            dve.wait_ge(act_in, 3)
            step(nc.vector.scalar_tensor_tensor(out=h[:], in0=tmp[:], scalar=0.0, in1=over_b(rw("alpha")),
                                                op0=ALU.min, op1=ALU.mult))
            dve.wait_ge(act_out, 3)
            step(nc.vector.tensor_tensor(h[:], h[:], tmp2[:], ALU.add))

            def layer_norm(source, turn):
                step(nc.vector.tensor_reduce(small[:, 0, :], source, AX.X, ALU.add))
                step(nc.vector.tensor_scalar(small[:, 4, :], small[:, 0, :], 1.0 / C, None, ALU.mult))
                nc.vector.tensor_tensor(tmp[:], source, over_c(small[:, 4, :]), ALU.subtract).then_inc(act_in, 1)
                dve.wait_ge(act_out, turn)
                step(nc.vector.tensor_reduce(small[:, 0, :], tmp2[:], AX.X, ALU.add))
                root(small[:, 0, :], 1.0 / C, LN_EPS, turn + 1)

            layer_norm(h[:], 4)
            for k in range(4):
                b = slice(4 * k, 4 * k + 4)
                for i in range(2):
                    ins = nc.vector.tensor_tensor(xn2x[:, b, i, :], tmp[:, b, :],
                                                  small[:, 5, b].unsqueeze(2).to_broadcast([P, 4, C]), ALU.mult)
                ins.then_inc(xn_ready, 1)

            for k in range(4):
                dve.wait_ge(xt_ready, k + 1)
                for parity in range(2):
                    half = slice(C * parity, C * parity + C)
                    src = XT[half, 4 * k:4 * k + 4, :].rearrange("p b (g j i) -> p i b j g", g=TQ, i=2)[:, parity, :, :, :]
                    nc.vector.tensor_scalar(neg_x[half, 4 * k:4 * k + 4, :, :], src, -1.0, None,
                                            ALU.mult).then_inc(neg_x_ready, 1)

            def save_q(G):
                for turn in range(2):
                    dve.wait_ge(qp_ready, G * 2 + (turn + 1))
                    for bank in range(2):
                        for k in range(2):
                            hd = 4 * bank + 2 * turn + k
                            ins = nc.vector.tensor_scalar(
                                qn[:, hd, :, :],
                                ps[:, 4 + 2 * turn + bank, k * GC:(k + 1) * GC].rearrange("p (b t) -> p b t", b=BG),
                                cst("bq")[:, hd:hd + 1], inv_wk[:, hd:hd + 1], ALU.add, ALU.mult)
                    ins.then_inc(q_ready, 1)

            def pieces(G, J):
                for half in range(2):
                    dve.wait_ge(half_free, G * NHALF + J * 2 + (half + 1))
                    for g, b in PIECES:
                        if (g, b) not in ACT_PIECES:
                            piece = relu_piece(nc.vector, G, J, half, g, b)
                    piece.then_inc(dve_half, 1)

            def group(G, last):
                with dve.Fori(1, NJ // 2) as J:
                    pieces(G, J)
                if not last:
                    dve.wait_ge(act_half, G * NHALF + NHALF)
                    save_q(G + 1)
                for b in range(BG):
                    dve.wait_ge(vp_ready, G * BG + (BG + b + 1))
                    nc.vector.tensor_tensor(V[:, b, :, :], ps[:, 4 + 2 * b:6 + 2 * b, :],
                                            rw("bv").rearrange("p (d n) -> p d n", d=2), ALU.add).then_inc(v_ready, 1)
                for k in range(BANKS):
                    hs = slice(HEADS_PER_BANK * k, HEADS_PER_BANK * (k + 1))
                    dve.wait_ge(e_ready, G * BANKS + (k + 1))
                    nc.vector.tensor_scalar(den1[:, hs, :], den[:, hs, :], 1.0, None, ALU.add).then_inc(norm_step, 1)
                    dve.wait_ge(norm_step, G * (2 * BANKS) + (2 * k + 1))
                    nc.vector.reciprocal(rden[:, hs, :], den1[:, hs, :]).then_inc(norm_step, 1)
                    dve.wait_ge(norm_step, G * (2 * BANKS) + (2 * k + 2))
                    nc.vector.tensor_tensor(A[:, hs, :, :], A[:, hs, :, :],
                                            rden[:, hs, :].unsqueeze(3).to_broadcast([P, HEADS_PER_BANK, BG, T]),
                                            ALU.mult).then_inc(a_ready, 1)

            def save_o(G):
                dve.wait_ge(o_done, G + 1)
                nc.vector.tensor_copy(OT[:].rearrange("p g t -> p (g t)")[:, bass.ds(G * T, T)],
                                      ps[:, 6, 0:T]).then_inc(o_saved, 1)

            save_q(0)
            dve.wait_ge(xw_psum, 1)
            nc.vector.tensor_copy(neg_xw[:], ps[:, 4, 0:NB * NH].rearrange("p (b h) -> p b h", b=NB)).then_inc(xw_ready, 1)
            dve.wait_ge(q_ready, 2)
            pieces(0, 0)
            with dve.Fori(0, NG - 1) as G:
                group(G, False)
                dve.wait_ge(q_ready, G * 2 + 4)
                pieces(G + 1, 0)
                save_o(G)
            group(NG - 1, True)
            save_o(NG - 1)

            for n in range(2):
                gs = slice(n * GH, (n + 1) * GH)
                dve.wait_ge(gate_ready, n + 1)
                nc.vector.tensor_tensor(yT[:, gs, :], OT[:, gs, :], gate[:, gs, :], ALU.mult).then_inc(y_ready, 1)
            dve.wait_ge(base_ready, 1)
            for n in range(2):
                dve.wait_ge(fan_done, n + 1)
                step(nc.vector.tensor_tensor(h[:, bs(n), :], base[:, bs(n), :],
                                             ps[:, n, :].rearrange("p (b c) -> p b c", b=NB // 2), ALU.add))
            step(nc.vector.tensor_reduce(small[:, 0, :], h[:], AX.X, ALU.add))
            step(nc.vector.tensor_scalar(small[:, 4, :], small[:, 0, :], 1.0 / C, None, ALU.mult))
            for n in range(2):
                nc.vector.tensor_tensor(tmp[:, bs(n), :], h[:, bs(n), :],
                                        small[:, 4, bs(n)].unsqueeze(2).to_broadcast([P, NB // 2, C]),
                                        ALU.subtract).then_inc(centred, 1)
            for n in range(2):
                dve.wait_ge(squared, n + 1)
                step(nc.vector.tensor_reduce(small[:, 0, bs(n)], tmp2[:, bs(n), :], AX.X, ALU.add))
            root(small[:, 0, :], 1.0 / C, LN_EPS, 6)
            for n in range(2):
                nc.vector.tensor_tensor(tmp[:, bs(n), :], tmp[:, bs(n), :],
                                        small[:, 5, bs(n)].unsqueeze(2).to_broadcast([P, NB // 2, C]),
                                        ALU.mult).then_inc(x2_ready, 1)

            def over_e(ap):
                return ap.unsqueeze(2).to_broadcast([P, NB, NE])

            dve.wait_ge(logit_psum, 1)
            step(nc.vector.tensor_tensor(rt[:, 4], ps[:, 6, 0:NB * NE].rearrange("p (b e) -> p b e", e=NE),
                                         rw("rb2").unsqueeze(1).to_broadcast([P, NB, NE]), ALU.add))
            step(nc.vector.tensor_reduce(small[:, 6, :], rt[:, 4], AX.X, ALU.max))
            nc.vector.tensor_tensor(rt[:, 0], rt[:, 4], over_e(small[:, 6, :]), ALU.subtract).then_inc(act_in, 1)
            dve.wait_ge(act_out, 7)
            step(nc.vector.tensor_reduce(small[:, 6, :], rt[:, 1], AX.X, ALU.add))
            step(nc.vector.reciprocal(small[:, 7, :], small[:, 6, :]))
            nc.vector.tensor_tensor(rt[:, 2], rt[:, 1], over_e(small[:, 7, :]), ALU.mult).then_inc(act_in, 1)
            dve.wait_ge(act_in, 8)
            mine = rt[:, 2].unsqueeze(3).to_broadcast([P, NB, NE, NE])
            other = rt[:, 2].unsqueeze(2).to_broadcast([P, NB, NE, NE])
            lower = rw("lower").rearrange("p (e f) -> p e f", e=NE).unsqueeze(1).to_broadcast([P, NB, NE, NE])
            step(nc.vector.tensor_tensor(rank6[:, 0], other, mine, ALU.is_equal))
            step(nc.vector.tensor_tensor(rank6[:, 0], rank6[:, 0], lower, ALU.mult))
            step(nc.vector.tensor_tensor(rank6[:, 1], other, mine, ALU.is_gt))
            step(nc.vector.tensor_tensor(rank6[:, 0], rank6[:, 0], rank6[:, 1], ALU.add))
            step(nc.vector.tensor_reduce(rt[:, 5], rank6[:, 0], AX.X, ALU.add))
            step(nc.vector.tensor_scalar(rt[:, 6], rt[:, 5], 1.5, None, ALU.is_lt))
            dve.wait_ge(act_out, 8)
            step(nc.vector.tensor_tensor(rt[:, 6], rt[:, 6], rt[:, 3], ALU.mult))
            step(nc.vector.tensor_reduce(small[:, 6, :], rt[:, 6], AX.X, ALU.add))
            step(nc.vector.reciprocal(small[:, 7, :], small[:, 6, :]))
            step(nc.vector.tensor_tensor(rt[:, 7], rt[:, 6], over_e(small[:, 7, :]), ALU.mult))
            pair = rt[:, 7].rearrange("p (g i) e -> p g (i e)", i=BG)
            part = part_b[:].rearrange("p (g n) -> p g n", g=NG)
            step(nc.vector.tensor_copy(part, pair))
            step(nc.vector.tensor_copy(cw[:, :, 0, :], part))
            step(nc.vector.tensor_tensor(pair, pair, cw[:, :, 0, :], ALU.subtract))
            step(nc.vector.tensor_copy(part, pair))
            step(nc.vector.tensor_copy(cw[:, :, 1, :], part))
            nc.vector.tensor_tensor(cw[:, :, 2, :], pair, cw[:, :, 1, :], ALU.subtract).then_inc(cw_ready, 1)

            for u, (n, e) in enumerate(UNITS):
                dve.wait_ge(h2_ready, u + 1)
                if u >= 2:
                    dve.wait_ge(y_psum, u - 1)
                nc.vector.tensor_tensor(H2c[:, u % 2, :], H2[:, u % 2, :], ps[:, 4 + u % 2, :],
                                        ALU.mult).then_inc(h2c_ready, 1)
                if u in (NE + 1, len(UNITS) - 1):
                    dve.wait_ge(y_psum, NE * (n + 1) if u > NE + 1 else NE)
                    done = n if u > NE + 1 else 0
                    nc.vector.tensor_tensor(result[:, bs(done), :], h[:, bs(done), :],
                                            ps[:, 6 + done, :].rearrange("p (b c) -> p b c", b=NB // 2),
                                            ALU.add).then_inc(result_ready, 1)

        @block.tensor
        def _(pe):
            pe.sem_inc(half_free, 2)
            pe.sem_inc(vp_ready, BG)

            pe.wait_ge(pool_step, 1)
            pe.wait_ge(conv_ready, 1)
            pe.wait_ge(rows_loaded, 16)
            for g in range(NG):
                if g % LOAD_G == 0:
                    pe.wait_ge(x_loaded[g // LOAD_G], 16)
                where = ps[:, g // GH, (g % GH) * P:(g % GH + 1) * P]
                for k in range(TAPS):
                    nc.tensor.matmul(where, xc[:, g, k:k + T_IN:2], conv[:, k, :],
                                     start=(k == 0 and g % GH == 0), stop=False, skip_group_check=True)
                ins = nc.tensor.matmul(where, ones[0:1, :], rw("conv_b")[0:1, :], start=False, stop=True,
                                       skip_group_check=True)
                if g % GH == GH - 1:
                    ins.then_inc(conv_done, 1)
            for k in range(2):
                pe.wait_ge(stat_ready, k + 1)
                nc.tensor.matmul(ps[:, 2, k * NB:(k + 1) * NB], ones[:], small[:, 0, :], start=(k == 0), stop=True,
                                 skip_group_check=True).then_inc(stat_summed, 1)
            for b in range(NB):
                pe.wait_ge(xn_ready, b // 4 + 1)
                ins = nc.tensor.transpose(ps[:, b // 4, (b % 4) * T:(b % 4 + 1) * T],
                                          xn2x[:, b, :, :].rearrange("p i c -> p (i c)"), ident)
                if b % 4 == 3:
                    ins.then_inc(xt_psum, 1)
            def project_q(x):
                for turn in range(2):
                    for k in range(2):
                        for half in range(2):
                            rows = slice(C * half, C * half + C)
                            ins = nc.tensor.matmul(ps[:, 4 + 2 * turn + half, k * GC:(k + 1) * GC],
                                                   wq[rows, 2 * turn + k, :],
                                                   x[rows, :, :],
                                                   start=(k == 0), stop=True, skip_group_check=True)
                    ins.then_inc(qp_ready, 1)

            def start_distances(G):
                pe.wait_ge(q_ready, G * 2 + 2)
                for hd in range(NH):
                    nc.tensor.matmul(R[:, hd, :], start_w[:, hd, :], qn[:, hd, :, :],
                                     start=(hd % HEADS_PER_BANK == 0), stop=False, skip_group_check=True)

            def group(G, last):
                with pe.Fori(0, NJ // 2) as J:
                    for half in range(2):
                        pe.wait_ge(win_ready, G * NHALF + J * 2 + (half + 1))
                        pe.wait_ge(dve_half, G * NHALF + J * 2 + (half + 1))
                        pe.wait_ge(act_half, G * NHALF + J * 2 + (half + 1))
                        for hd in range(NH):
                            for g in range(TQ):
                                ins = nc.tensor.matmul(R[32 * g:32 * g + 32, hd, :], window[:, half, hd, :],
                                                       D[:, half, g, hd * GC:(hd + 1) * GC],
                                                       start=False, stop=False, skip_group_check=True,
                                                       tile_position=(0, 32 * g))
                        ins.then_inc(half_free, 1)
                pe.wait_ge(x_copied, G + 1)
                if not last:
                    project_q(x_next)
                for b in range(BG):
                    if last:
                        pe.wait_ge(q_ready, G * 2 + 2)
                    else:
                        pe.wait_ge(q_ready, G * 2 + (3 + b))
                    for half in range(2):
                        rows = slice(C * half, C * half + C)
                        ins = nc.tensor.matmul(ps[:, 4 + 2 * b + half, :], x_now[rows, b, :], wv[rows, :],
                                               start=True, stop=True)
                    ins.then_inc(vp_ready, 1)
                if not last:
                    pe.wait_ge(e_ready, G * BANKS + BANKS)
                    start_distances(G + 1)
                pe.wait_ge(v_ready, G * BG + BG)
                for k in range(BANKS):
                    pe.wait_ge(a_ready, G * BANKS + (k + 1))
                    if k >= 2:
                        pe.wait_ge(at_ready, G * BANKS + (k - 1))
                    for n in range(HEADS_PER_BANK * BG):
                        ins = nc.tensor.transpose(ps[:, 4 + k % 2, n * T:(n + 1) * T],
                                                  A[:, 2 * k + n // 2, n % 2, :], ident)
                    ins.then_inc(tp_ready, 1)
                for k in range(BANKS):
                    pe.wait_ge(at_ready, G * BANKS + (k + 1))
                    for hd in range(HEADS_PER_BANK * k, HEADS_PER_BANK * (k + 1)):
                        for d in range(2):
                            for b in range(BG):
                                attn = (AT, A)[d]
                                ins = nc.tensor.matmul(ps[C * b:C * b + C, 6, 0:T],
                                                       V[:, b, d, hd * C:(hd + 1) * C], attn[:, hd, b, :],
                                                       start=(hd == 0 and d == 0), stop=(hd == NH - 1 and d == 1),
                                                       skip_group_check=True)
                ins.then_inc(o_done, 1)
                if not last:
                    pe.wait_ge(o_saved, G + 1)

            pe.wait_ge(xt_ready, 1)
            project_q(XT[:, 0:BG, :])
            pe.wait_ge(q_ready, 1)
            pe.wait_ge(xt_ready, 4)
            for b in range(NB):
                ins = nc.tensor.matmul(ps[:, 4, b * NH:(b + 1) * NH], XT[0:C, b, :], wk8[0:C, :],
                                       start=(b == 0), stop=True, skip_group_check=True)
            ins.then_inc(xw_psum, 1)
            pe.wait_ge(pool_step, 5)
            start_distances(0)
            pe.wait_ge(xw_ready, 1)
            with pe.Fori(0, NG - 1) as G:
                group(G, False)
            group(NG - 1, True)

            pe.wait_ge(const2_loaded, 16)
            for n in range(2):
                pe.wait_ge(y_ready, n + 1)
                for g in range(GH):
                    ins = nc.tensor.matmul(ps[:, n, g * P:(g + 1) * P], yT[:, n * GH + g, :], cst("fan"),
                                           start=(g == 0), stop=True, skip_group_check=True)
                ins.then_inc(fan_done, 1)
            for n in range(2):
                pe.wait_ge(x2_ready, n + 1)
                for g in range(GH):
                    b = BG * (n * GH + g)
                    ins = nc.tensor.transpose(ps[:, 2 + n, g * P:(g + 1) * P],
                                              tmp[:, b:b + BG, :].rearrange("p b c -> p (b c)"), ident)
                ins.then_inc(x2t_psum, 1)
            for n in range(2):
                pe.wait_ge(x2t_ready, n + 1)
                nc.tensor.matmul(ps[0:BG * RH, 4 + n, :], cst("rw1"), X2T[:, n * GH:(n + 1) * GH, :],
                                 start=True, stop=True).then_inc(rh_psum, 1)
            for g in range(NG):
                pe.wait_ge(rh_ready, g // GH + 1)
                ins = nc.tensor.matmul(ps[:, 6, g * BG * NE:(g + 1) * BG * NE], rhT[0:BG * RH, g, :],
                                       cst("rw2")[0:BG * RH, :], start=(g == 0), stop=True, skip_group_check=True)
            ins.then_inc(logit_psum, 1)

            def first_layer(u):
                n, e = UNITS[u]
                if u >= 2:
                    pe.wait_ge(h1_ready, u - 1)
                nc.tensor.matmul(ps[:, u % 2, :], cst("w1")[:, e * P:(e + 1) * P], X2T[:, n * GH:(n + 1) * GH, :],
                                 start=True, stop=True).then_inc(h1_psum, 1)

            def second_layer(u):
                n, e = UNITS[u]
                if u >= 2:
                    pe.wait_ge(h2c_ready, u - 1)
                nc.tensor.matmul(ps[:, 4 + u % 2, :], pick_b[0:CK, e * P:(e + 1) * P],
                                 cwT_b[0:CK, n * GH:(n + 1) * GH, :], start=True, stop=True)
                pe.wait_ge(h1_ready, u + 1)
                nc.tensor.matmul(ps[:, 2 + u % 2, :], cst("w2")[:, e * P:(e + 1) * P], H1[:, u % 2, :],
                                 start=True, stop=True).then_inc(h2_psum, 1)

            def third_layer(u):
                n, e = UNITS[u]
                if e == 0:
                    for g in range(GH):
                        nc.tensor.matmul(ps[:, 6 + n, g * P:(g + 1) * P], cwT[0:CK, n * GH + g, :],
                                         cst("b3")[0:CK, :], start=(g == 0), stop=False, skip_group_check=True)
                pe.wait_ge(h2c_ready, u + 1)
                for g in range(GH):
                    ins = nc.tensor.matmul(ps[:, 6 + n, g * P:(g + 1) * P], H2c[:, u % 2, g * T:(g + 1) * T],
                                           cst("w3")[:, e * P:(e + 1) * P], start=False, stop=(e == NE - 1),
                                           skip_group_check=True)
                ins.then_inc(y_psum, 1)

            first_layer(0)
            first_layer(1)
            pe.wait_ge(cw_ready, 1)
            for g in range(NG):
                ins = nc.tensor.transpose(ps[0:CK, 6 + g // GH, (g % GH) * T:(g % GH + 1) * T],
                                          cw[:, g, :, :].rearrange("p k n -> p (k n)"), ident)
                if g % GH == GH - 1:
                    ins.then_inc(cwt_psum, 1)
            pe.wait_ge(cwt_ready, 4)
            pe.wait_ge(pick_ready, 1)
            for u in range(len(UNITS) + 1):
                if u < len(UNITS):
                    if u >= 1 and u + 1 < len(UNITS):
                        first_layer(u + 1)
                    second_layer(u)
                if u >= 1:
                    third_layer(u - 1)


def _pack(inputs):
    import numpy as np

    g = {k: np.asarray(v) for k, v in inputs.items()}
    dt = g["x"].dtype
    x_t = np.zeros((BG, C, NG, X_ROWS), dt)
    x_t[:, :, :, 1:T_IN + 1] = g["x"].reshape(NG, BG, T_IN, C).transpose(1, 3, 0, 2)

    packed = [np.zeros((P, NCOLS), dt), np.zeros((P, NCOLS2), dt)]

    def put(name, rows, value):
        k, a, b = COLS[name]
        packed[k][rows, a:b] = value.reshape(value.shape[0], -1)

    def put_block(name, rows, n, i, value):
        k, a, _ = COLS[name]
        a += BG * value.shape[1] * n + value.shape[1] * i
        packed[k][rows, a:a + value.shape[1]] = value

    wqv_t = g["L0_attn_wqv_w"].T
    q_t = wqv_t[:, :NH * C].reshape(C, NH, 1, C)
    q_t = np.concatenate([q_t, q_t], axis=2)
    v_t = wqv_t[:, NH * C:]
    put("ident", slice(0, P), np.eye(P, dtype=dt))
    for i in range(BG):
        rows = slice(C * i, C * i + C)
        put("conv_w", rows, g["L0_tok_w"].reshape(TAPS, C).T)
        put("wk", rows, g["L0_attn_wk"].T)
        put("bq", rows, g["L0_attn_wqv_b"][:NH * C].reshape(NH, C).T)
        put("wq", rows, q_t[:, 4 * i:4 * i + 4])
        put("wv", rows, v_t[:, NH * C * i:NH * C * (i + 1)])
        put("b1", rows, g["L0_ffn_expert_b1"].T)
        put("b2", rows, g["L0_ffn_expert_b2"].T)
        put("rb1", slice(RH * i, RH * i + RH), g["L0_ffn_router_b1"].reshape(RH, 1))
        put_block("fan", rows, 0, i, g["L0_attn_fanin_w"].T)
        put_block("rw1", rows, 0, i, g["L0_ffn_router_w1"])
        put_block("rw2", slice(RH * i, RH * i + RH), 0, i, g["L0_ffn_router_w2"])
        for e in range(NE):
            put_block("w1", rows, e, i, g["L0_ffn_expert_w1"][e])
            put_block("w2", rows, e, i, g["L0_ffn_expert_w2"][e])
            put_block("w3", rows, e, i, g["L0_ffn_expert_w3"][e])
            for part in range(PARTS):
                one = (part * BG + i) * NE + e
                put_block("pick", slice(one, one + 1), e, i, np.ones((1, C), dt))
        for part in range(PARTS):
            put_block("b3", slice((part * BG + i) * NE, (part * BG + i + 1) * NE), 0, i, g["L0_ffn_expert_b3"])

    lower = np.tril(np.ones((NE, NE), dt), -1)
    conv_b = g["L0_tok_b"]
    parts = {"conv_b": np.concatenate([conv_b, conv_b]), "gamma": g["L0_tok_gamma"], "beta": g["L0_tok_beta"],
             "alpha": g["L0_tok_alpha"], "fan_b": g["L0_attn_fanin_b"], "bv": g["L0_attn_wqv_b"][NH * C:],
             "rb2": g["L0_ffn_router_b2"], "lower": lower}
    rows = np.concatenate([parts[name].reshape(-1) for name in ROWS]).reshape(NROWS)
    return {"x_t": x_t.reshape(P, NG, X_ROWS), "cols": packed[0], "cols2": packed[1], "rows": rows}


def kernel(**inputs):
    import concourse.bacc as _bacc
    from concourse.bass_utils import run_bass_kernel_spmd as _run

    arrays = _pack(inputs)
    nc = _bacc.Bacc("TRN2", target_bir_lowering=False, num_devices=1)
    args = [nc.dram_tensor(name, a.shape, mybir.dt.from_np(a.dtype), kind="ExternalInput").ap()
            for name, a in arrays.items()]
    out = nc.dram_tensor("out", (NB, T, C), F32, kind="ExternalOutput").ap()
    build(nc, *args, out)
    return _run(nc, [arrays], core_ids=[0]).results[0]["out"]
```

```python
from contextlib import ExitStack

import concourse.bass as bass
from concourse import mybir

F32 = mybir.dt.float32
BF16 = mybir.dt.bfloat16
ALU = mybir.AluOpType
ACT = mybir.ActivationFunctionType
AX = mybir.AxisListType

NB, T_IN, C = 16, 256, 64
TAPS = 5
T = T_IN // 2
NH = 8
P = 128
BG = 2
NG = NB // BG
GC = BG * T
TQ = 4
NJ = 32 // 2
HEADS_PER_BANK = 512 // GC
NE, RH = 6, 32
TINY = 1e-30
CONV_EPS, LN_EPS = 1e-3, 1e-5
X_ROWS = T_IN + 4
LOADS = ((0, 1), (1, 2), (2, 4), (4, NG))
GH = NG // 2
EARLY = (slice(0, BG), slice(BG, NB))
LATE = (slice(0, NB - BG), slice(NB - BG, NB))
PARTS = 3
PART_ROWS = (0, 64, 96)
CK = PARTS * BG * NE

COLS = {}
for _names in ([("ident", P), ("conv_w", TAPS), ("wk", NH), ("bq", NH), ("wq", 4 * 2 * C),
                ("wk_q", 4 * C), ("wv", NH * C)],
               [("fan", P), ("rw1", BG * RH), ("rw2", BG * NE), ("rb1", 1), ("b1", NE), ("b2", NE), ("b3", P),
                ("w1", NE * P), ("w2", NE * P), ("w3", NE * P), ("pick", NE * P)]):
    _at = 0
    for _name, _n in _names:
        COLS[_name] = (len(_names) > 7, _at, _at + _n)
        _at += _n
    if len(_names) > 7:
        NCOLS2 = _at
    else:
        NCOLS = _at
ROWS = {}
_at = 0
for _name, _n in [("conv_b", NB // 2 * C), ("gamma", C), ("beta", C), ("alpha", C), ("fan_b", C),
                  ("rb2", NE), ("lower", NE * NE), ("bv", 2 * NH * C)]:
    ROWS[_name] = (_at, _at + _n)
    _at += _n
NROWS = _at


def build(nc, x_t, cols, cols2, rows, out):
    with ExitStack() as ctx:
        def sb(name, shape):
            return ctx.enter_context(nc.sbuf_tensor(name, shape, F32))

        def sem(name):
            return ctx.enter_context(nc.semaphore(name))

        const = [sb("const", [P, NCOLS]), sb("const2", [P, NCOLS2])]
        row = sb("row", [P, NROWS])
        xc = sb("xc", [P, NG, X_ROWS])
        conv = sb("conv", [P, TAPS, P])
        pick_b = ctx.enter_context(nc.sbuf_tensor("pick_b", [P, NE * P], BF16))
        part_b = ctx.enter_context(nc.sbuf_tensor("part_b", [P, NB * NE], BF16))
        cwT_b = ctx.enter_context(nc.sbuf_tensor("cwT_b", [P, NG, T], BF16))
        h = sb("h", [P, NB, C])
        base = sb("base", [P, NB, C])
        xn2x = sb("xn2x", [P, NB, 2, C])
        tmp = sb("tmp", [P, NB, C])
        tmp2 = sb("tmp2", [P, NB, C])
        small = sb("small", [P, 8, NB])
        minus_half = sb("minus_half", [P, NB])
        cw = sb("cw", [P, NG, PARTS, BG * NE])
        ones = sb("ones", [P, P])
        XT = sb("XT", [P, NB, T])
        x_now = sb("x_now", [P, BG, T])
        x_next = sb("x_next", [P, BG, T])
        neg_x = sb("neg_x", [P, NB, NJ, TQ])
        neg_xw = sb("neg_xw", [P, NB, NH])
        abs_wk = sb("abs_wk", [P, NH])
        sgn_wk = sb("sgn_wk", [P, NH])
        inv_wk = sb("inv_wk", [P, NH])
        wk8 = sb("wk8", [P, NH])
        sum_wq = sb("sum_wq", [P, P])
        sum_bq = sb("sum_bq", [P, P])
        sum_b = sb("sum_b", [P, 1])
        sum_q = sb("sum_q", [P, 4])
        half_sgn = sb("half_sgn", [P, 4, C])
        rest = sb("rest", [P, GC])
        bv_parts = ctx.enter_context(nc.sbuf_tensor("bv_parts", [P, 2 * NH * C], BF16))
        bv_rest = sb("bv_rest", [P, 2 * NH * C])
        opening = ctx.enter_context(nc.sbuf_tensor("opening", [P, GC], BF16))
        head_row = ctx.enter_context(nc.sbuf_tensor("head_row", [P, NH, P], BF16))
        hot = sb("hot", [P, NH, 62])
        window = sb("window", [P, 2, NH, 32])
        qn = sb("qn", [P, NH, BG, T])
        D = sb("D", [P, 2, TQ, NH * GC])
        V = sb("V", [P, BG, 2, NH * C])
        A = sb("A", [P, NH, BG, T])
        AT = sb("AT", [P, NH, BG, T])
        den = sb("den", [P, NH, BG])
        den1 = sb("den1", [P, NH, BG])
        rden = sb("rden", [P, NH, BG])
        OT = sb("OT", [P, NG, T])
        ps = ctx.enter_context(nc.psum_tensor("ps", [P, 8, 512], F32))
        R = ps[:, 0:4, :].rearrange("p k (h n) -> p (k h) n", n=GC)

        def cst(name):
            k, a, b = COLS[name]
            return const[k][:, a:b]

        QV_AT = COLS["wq"][1]
        BV_AT = ROWS["bv"][0]
        AT_BANK = 2
        XT_BANK, XT_BANKS = (6, 4), 4
        FAN_BANK, X2T_BANK, RH_BANK, CWT_BANK = (4, 7), (6, 7), (4, 7), (2, 7)

        def conv_psum(n):
            return ps[:, 4, 0:BG * C] if n == 0 else ps[:, 0:2, :].rearrange("p k n -> p (k n)")[:, 0:(NB - BG) * C]

        def late_psum(n, banks):
            k = banks[n]
            return ps[:, k, 0:BG * C] if n else ps[:, k:k + 2, :].rearrange("p k n -> p (k n)")[:, 0:(NB - BG) * C]

        def rw(name):
            a, b = ROWS[name]
            return row[:, a:b]

        def size(b):
            return b.stop - b.start

        def groups(b):
            return range(b.start // BG, b.stop // BG)

        def gsl(b):
            return slice(b.start // BG, b.stop // BG)

        def unit(n):
            return slice(n * GH, (n + 1) * GH)

        def halves(b):
            m = b.start + (size(b) + 1) // 2
            return slice(b.start, m), slice(m, b.stop)

        def flat(ap):
            return ap.rearrange("p a b -> p (a b)")

        ident = cst("ident")
        wq = cst("wq").rearrange("p (m n) -> p m n", m=4)
        wv = cst("wv")
        xc_flat = flat(xc[:])
        X2T = xc_flat[:, 0:NG * T].rearrange("p (g t) -> p g t", g=NG)
        rhT = xc_flat[:, NG * T:2 * NG * T].rearrange("p (g t) -> p g t", g=NG)
        xn_flat = xn2x[:].rearrange("p b i c -> p (b i c)")
        cwT = xn_flat[:, 0:NG * T].rearrange("p (g t) -> p g t", g=NG)
        rt = xn_flat[:, NG * T:NG * T + 8 * NB * NE].rearrange("p (k b e) -> p k b e", k=8, e=NE)
        rank = D[:, 0, 2, 0:2 * NB * NE * NE].rearrange("p (k b e f) -> p k b e f", k=2, e=NE, f=NE)
        D_flat = D[:, 0, :, :].rearrange("p g n -> p (g n)")
        H1 = D_flat[:, 0:1024].rearrange("p (k n) -> p k n", k=2)
        H2 = D_flat[:, 1024:2048].rearrange("p (k n) -> p k n", k=2)
        H2c = D_flat[:, 2048:3072].rearrange("p (k n) -> p k n", k=2)
        result = D_flat[:, 3072:4096].rearrange("p (b c) -> p b c", b=NB)

        def pair(name):
            return [sem(name + "_a"), sem(name + "_b")]

        const_loaded, const2_loaded, rows_loaded = sem("const_loaded"), sem("const2_loaded"), sem("rows_loaded")
        qv_loaded, bv_loaded = sem("qv_loaded"), sem("bv_loaded")
        x_loaded = [sem(f"x_loaded{i}") for i in range(len(LOADS))]
        dve_step = sem("dve_step")
        pool_step = sem("pool_step")
        wk_ready, conv_ready = sem("wk_ready"), sem("conv_ready")
        conv_done = pair("conv_done")
        conv_saved = sem("conv_saved")
        sum_in, sum_out = pair("sum_in"), pair("sum_out")
        centred, squared = pair("centred"), pair("squared")
        var_ready, root_ready = pair("var_ready"), pair("root_ready")
        yn_ready, pos_ready = pair("yn_ready"), pair("pos_ready")
        xn_ready, xt_psum, xt_ready = pair("xn_ready"), pair("xt_psum"), pair("xt_ready")
        neg_x_ready, xw_psum, xw_ready = pair("neg_x_ready"), pair("xw_psum"), pair("xw_ready")
        base_ready = sem("base_ready")
        x_copied = sem("x_copied")
        qp_ready = sem("qp_ready")
        q_ready = sem("q_ready")
        sums_ready = sem("sums_ready")
        sum_b_psum, sum_b_ready = sem("sum_b_psum"), sem("sum_b_ready")
        rows_ready = sem("rows_ready")
        qsum_psum = sem("qsum_psum")
        first_part = sem("first_part")
        rest_ready = sem("rest_ready")
        opening_ready = sem("opening_ready")
        vp_ready = sem("vp_ready")
        v0_ready, v1_ready = sem("v0_ready"), sem("v1_ready")
        bv_first, bv_less, bv_second = sem("bv_first"), sem("bv_less"), sem("bv_second")
        bv_ready = sem("bv_ready")
        win_ready = sem("win_ready")
        dve_half, act_half = sem("dve_half"), sem("act_half")
        half_free = sem("half_free")
        e_ready = sem("e_ready")
        norm_step = sem("norm_step")
        a_ready = sem("a_ready")
        tp_ready, at_ready = sem("tp_ready"), sem("at_ready")
        o_done, o_saved = sem("o_done"), sem("o_saved")
        gate_ready, y_ready, fan_done = pair("gate_ready"), pair("y_ready"), pair("fan_done")
        x2_ready, x2t_psum, x2t_ready = pair("x2_ready"), pair("x2t_psum"), pair("x2t_ready")
        rh_psum, rh_ready, logit_psum = pair("rh_psum"), pair("rh_ready"), pair("logit_psum")
        logit_read = sem("logit_read")
        exp_in, exp_out = pair("exp_in"), pair("exp_out")
        pick_ready = sem("pick_ready")
        cw_ready, cwt_psum, cwt_ready = pair("cw_ready"), pair("cwt_psum"), pair("cwt_ready")
        h1_psum, h1_ready = sem("h1_psum"), sem("h1_ready")
        h2_psum, h2_ready = sem("h2_psum"), sem("h2_ready")
        h2c_ready = sem("h2c_ready")
        y_psum, result_ready, stored = sem("y_psum"), sem("result_ready"), sem("stored")

        NHALF = NJ
        STEPS = NJ // 2
        BANKS = 4
        ACT_PIECES = ((0, 1), (2, 1), (3, 1))
        PIECES = [(g, b) for g in range(TQ) for b in range(BG)]
        UNITS = [(n, e) for n in range(2) for e in range(NE)]

        block = ctx.enter_context(nc.Block())

        @block.sync
        def _(sp):
            sp.dma_start(const[0][:, 0:QV_AT], cols[:, 0:QV_AT]).then_inc(const_loaded, 16)
            for k, (first, end) in enumerate(LOADS):
                g = slice(first, end)
                sp.dma_start(xc[:, g, :], x_t[:, g, :]).then_inc(x_loaded[k], 16)
            sp.dma_start(const[1][:], cols2).then_inc(const2_loaded, 16)
            for n in range(2):
                sp.wait_ge(result_ready, n + 1)
                b = slice(n * BG * GH, (n + 1) * BG * GH)
                sp.dma_start(out[b].rearrange("b t c -> t b c"), result[:, b, :]).then_inc(stored, 16)
            sp.wait_ge(stored, 32)

        @block.gpsimd
        def _(pool):
            steps = [0]

            def step(ins):
                steps[0] += 1
                ins.then_inc(pool_step, 1)
                pool.wait_ge(pool_step, steps[0])

            def root(n, turn):
                b = (EARLY, EARLY, LATE)[turn - 1][n]
                pool.wait_ge(var_ready[n], turn)
                nc.gpsimd.tensor_tensor(small[:, 5, b], small[:, 1, b], minus_half[:, b],
                                        ALU.pow).then_inc(root_ready[n], 1)

            def residual(part):
                if part == 0:
                    for n in range(2):
                        pool.wait_ge(xn_ready[n], 2)
                    pool.wait_ge(rows_loaded, 16)
                    step(nc.gpsimd.tensor_tensor(base[:], h[:], xn2x[:, :, 0, :], ALU.add))
                else:
                    nc.gpsimd.tensor_tensor(base[:], base[:], rw("fan_b").unsqueeze(1).to_broadcast([P, NB, C]),
                                            ALU.add).then_inc(base_ready, 1)

            def split_opening(G):
                pool.wait_ge(win_ready, G * NHALF + 2)
                pool.wait_ge(rest_ready, G + 1)
                nc.gpsimd.tensor_tensor(opening[96:P, :], rest[96:P, :], opening[96:P, :],
                                        ALU.subtract).then_inc(opening_ready, 1)

            def windows(G, J, halves=(0, 1)):
                for half in halves:
                    pool.wait_ge(half_free, G * NHALF + J * 2 + (half + 1))
                    nc.gpsimd.tensor_copy(window[:, half, :, :],
                                          hot[:, :, bass.ds(J * -4 + (30 - 2 * half), 32)]).then_inc(win_ready, 1)

            step(nc.gpsimd.memset(ones[:], 1.0))
            step(nc.gpsimd.memset(minus_half[:], -0.5))
            nc.gpsimd.memset(head_row[:], 0.0).then_inc(rows_ready, 1)
            pool.wait_ge(rows_ready, 1)
            step(nc.gpsimd.memset(hot[:], 0.0))
            pool.wait_ge(wk_ready, 1)
            step(nc.gpsimd.tensor_copy(hot[0:C, :, 30], abs_wk[0:C, :]))
            step(nc.gpsimd.tensor_copy(hot[C:P, :, 31], abs_wk[C:P, :]))
            windows(0, 0)
            pool.wait_ge(win_ready, 2)
            pool.wait_ge(bv_first, 1)
            nc.gpsimd.tensor_tensor(bv_rest[64:P, :], rw("bv")[64:P, :], bv_parts[64:P, :],
                                    ALU.subtract).then_inc(bv_less, 1)
            pool.wait_ge(bv_less, 1)
            root(0, 1)
            root(0, 2)
            pool.wait_ge(root_ready[0], 2)
            pool.wait_ge(bv_second, 1)
            nc.gpsimd.tensor_tensor(bv_parts[96:P, :], bv_rest[96:P, :], bv_parts[96:P, :],
                                    ALU.subtract).then_inc(bv_ready, 1)
            pool.wait_ge(bv_ready, 1)
            split_opening(0)
            pool.wait_ge(opening_ready, 1)
            root(1, 1)

            def copy_x(G, last):
                pool.wait_ge(vp_ready, G * BG + BG)
                pool.wait_ge(qsum_psum, G + 1)
                copy = nc.gpsimd.tensor_copy(flat(x_now[:]), flat(XT[:])[:, bass.ds(G * GC, GC)])
                if not last:
                    copy = nc.gpsimd.tensor_copy(flat(x_next[:]), flat(XT[:])[:, bass.ds(G * GC + GC, GC)])
                copy.then_inc(x_copied, 1)

            for k in range(2, NHALF):
                windows(0, k // 2, (k % 2,))
                if k == 9:
                    root(1, 2)
                if k in (12, 14):
                    residual((k - 12) // 2)
            for n in range(2):
                pool.wait_ge(xt_ready[n], (1, XT_BANKS)[n])
            copy_x(0, False)

            def between(G, last=False):
                copy_x(G + 1, last)
                for half in range(2):
                    nc.gpsimd.tensor_copy(window[:, half, :, :],
                                          hot[:, :, 30 - 2 * half:62 - 2 * half]).then_inc(win_ready, 1)
                split_opening(G + 1)

            between(0)
            with pool.Fori(1, NG - 2) as G:
                with pool.Fori(1, STEPS) as J:
                    windows(G, J)
                between(G)
            with pool.Fori(1, STEPS) as J:
                windows(NG - 2, J)
            between(NG - 2, True)
            pool.wait_ge(const2_loaded, 16)
            pool.wait_ge(opening_ready, NG)
            nc.gpsimd.tensor_copy(pick_b[:], cst("pick")).then_inc(pick_ready, 1)
            for k in range(2, NHALF):
                windows(NG - 1, k // 2, (k % 2,))
                if k == 9:
                    root(0, 3)
            root(1, 3)

        def relu_piece(engine, G, J, half, g, b):
            dst = D[:, half, g, :].rearrange("p (h b t) -> p h b t", h=NH, b=BG)[:, :, b, :]
            minus_x = neg_x[:].rearrange("p b j g -> p (b j g)")[
                :, bass.ds(G * (BG * NJ * TQ) + J * (2 * TQ) + (b * NJ * TQ + half * TQ + g), 1)]
            if engine is nc.scalar:
                return nc.scalar.activation(dst, qn[:, :, b, :], ACT.Relu, bias=minus_x)
            return nc.vector.tensor_scalar(dst, qn[:, :, b, :], minus_x, 0.0, ALU.add, ALU.max)

        @block.scalar
        def _(act):
            act.dma_start(row[:, 0:BV_AT], rows[0:BV_AT].partition_broadcast(P)).then_inc(rows_loaded, 16)
            act.dma_start(const[0][:, QV_AT:NCOLS], cols[:, QV_AT:NCOLS]).then_inc(qv_loaded, 16)
            act.dma_start(row[:, BV_AT:NROWS], rows[BV_AT:NROWS].partition_broadcast(P)).then_inc(bv_loaded, 16)

            def square(n, turn):
                b = (EARLY, EARLY, LATE)[turn - 1][n]
                act.wait_ge(centred[n], turn)
                nc.scalar.activation(tmp2[:, b, :], tmp[:, b, :], ACT.Square).then_inc(squared[n], 1)

            def positive(n):
                b = EARLY[n]
                act.wait_ge(yn_ready[n], 1)
                nc.scalar.activation(tmp2[:, b, :], tmp[:, b, :], ACT.Relu).then_inc(pos_ready[n], 1)

            def save_xt(n, banks):
                for k in banks:
                    act.wait_ge(xt_psum[n], 1)
                    b = slice(EARLY[n].start + 4 * k, min(EARLY[n].start + 4 * k + 4, EARLY[n].stop))
                    nc.scalar.activation(XT[:, b, :],
                                         ps[:, XT_BANK[n] + k, 0:size(b) * T].rearrange("p (b t) -> p b t", t=T),
                                         ACT.Copy).then_inc(xt_ready[n], 1)

            def gate(n):
                b = LATE[n]
                act.wait_ge(o_saved, gsl(b).stop + 1)
                nc.scalar.activation(flat(tmp2[:, b, :]), flat(OT[:, gsl(b), :]), ACT.Tanh,
                                     scale=0.851).then_inc(gate_ready[n], 1)

            def save_x2t(n):
                g = gsl(LATE[n])
                act.wait_ge(x2t_psum[n], 1)
                nc.scalar.activation(flat(X2T[:, g, :]), late_psum(n, X2T_BANK), ACT.Copy).then_inc(x2t_ready[n], 1)

            def router_hidden(n):
                g = gsl(LATE[n])
                act.wait_ge(rh_psum[n], 1)
                nc.scalar.activation(flat(rhT[0:BG * RH, g, :]), late_psum(n, RH_BANK)[0:BG * RH, :], ACT.Relu,
                                     bias=cst("rb1")[0:BG * RH, :]).then_inc(rh_ready[n], 1)

            def router_exp(n, turn):
                b = LATE[n]
                act.wait_ge(exp_in[n], turn)
                k = 2 * (turn - 1)
                nc.scalar.activation(rt[:, k + 1, b], rt[:, k, b], ACT.Exp).then_inc(exp_out[n], 1)

            def save_cwt(n):
                g = gsl(LATE[n])
                act.wait_ge(cwt_psum[n], 1)
                src = late_psum(n, CWT_BANK)[0:CK, :]
                nc.scalar.activation(flat(cwT_b[0:CK, g, :]), src, ACT.Copy).then_inc(cwt_ready[n], 1)
                nc.scalar.activation(flat(cwT[0:CK, g, :]), src, ACT.Copy).then_inc(cwt_ready[n], 1)

            def pieces(G, J, halves=(0, 1)):
                for half in halves:
                    act.wait_ge(half_free, G * NHALF + J * 2 + (half + 1))
                    for g, b in ACT_PIECES:
                        piece = relu_piece(nc.scalar, G, J, half, g, b)
                    piece.then_inc(act_half, 1)

            def first_opening(G, bank):
                act.wait_ge(qsum_psum, G + 1)
                nc.scalar.activation(opening[:], ps[:, bank, 0:GC], ACT.Identity, bias=sum_b[:]).then_inc(first_part, 1)

            def attention(G, last=False):
                act.wait_ge(half_free, G * NHALF + (NHALF + 2))
                for k in range(BANKS):
                    for hd in range(HEADS_PER_BANK * k, HEADS_PER_BANK * (k + 1)):
                        for b in range(BG):
                            e = nc.scalar.activation(
                                A[:, hd, b, :], R[:, hd, b * T:(b + 1) * T], ACT.Exp, scale=-0.25,
                                bias=flat(neg_xw[:])[:, bass.ds(G * (BG * NH) + (b * NH + hd), 1)],
                                accum_out=den[:, hd, b:b + 1])
                    e.then_inc(e_ready, 1)
                act.wait_ge(vp_ready, G * BG + 2 * BG)
                nc.scalar.activation(V[:, 1, :, :], ps[:, 6:8, :], ACT.Copy).then_inc(v1_ready, 1)
                if not last:
                    first_opening(G + 1, 0)
                for k in range(BANKS):
                    act.wait_ge(tp_ready, G * BANKS + (k + 1))
                    nc.scalar.activation(AT[:, 2 * k:2 * k + 2, :, :],
                                         ps[:, AT_BANK + k, :].rearrange("p (h b t) -> p h b t", h=2, b=BG),
                                         ACT.Copy).then_inc(at_ready, 1)

            act.wait_ge(const_loaded, 16)
            act.wait_ge(rows_ready, 1)
            for at in PART_ROWS:
                nc.scalar.activation(head_row[at:at + 32, :, :],
                                     ident[at:at + 32, at:at + NH].unsqueeze(2).to_broadcast([32, NH, P]),
                                     ACT.Copy).then_inc(rows_ready, 1)
            act.wait_ge(bv_loaded, 16)
            nc.scalar.activation(bv_parts[:], rw("bv"), ACT.Copy).then_inc(bv_first, 1)
            square(0, 1)
            act.wait_ge(bv_less, 1)
            nc.scalar.activation(bv_parts[64:P, :], bv_rest[64:P, :], ACT.Copy).then_inc(bv_second, 1)
            positive(0)
            square(0, 2)
            save_xt(0, (0,))
            act.wait_ge(sum_b_ready, 1)
            first_opening(0, 3)
            square(1, 1)
            nc.scalar.activation(small[:, 7, 0:1], ones[:, 0:1], ACT.Exp)
            act.wait_ge(neg_x_ready[0], 2)
            act.wait_ge(q_ready, 2)
            for k in range(NHALF):
                pieces(0, k // 2, (k % 2,))
                if k == 3:
                    positive(1)
                if k == 7:
                    square(1, 2)
                if k == 13:
                    save_xt(1, (0, 1))
                if k == 14:
                    save_xt(1, (2, 3))
            act.wait_ge(xw_ready[0], 1)
            attention(0)
            act.wait_ge(neg_x_ready[1], 4)
            act.wait_ge(xw_ready[1], 1)
            with act.Fori(1, NG - 1) as G:
                act.wait_ge(q_ready, G * 2 + 2)
                with act.Fori(0, STEPS) as J:
                    pieces(G, J)
                attention(G)
            act.wait_ge(q_ready, NG * 2)
            for k in range(NHALF):
                pieces(NG - 1, k // 2, (k % 2,))
                if k == 1:
                    gate(0)
                if k == 7:
                    square(0, 3)
                if k == 11:
                    save_x2t(0)
                if k == 13:
                    router_hidden(0)
            router_exp(0, 1)
            router_exp(0, 2)
            attention(NG - 1, True)
            save_cwt(0)

            def first_relu(u):
                act.wait_ge(h1_psum, u + 1)
                if u >= 2:
                    act.wait_ge(h2_psum, u - 1)
                nc.scalar.activation(H1[:, u % 2, :], ps[:, u % 2, :], ACT.Relu,
                                     bias=cst("b1")[:, UNITS[u][1]:UNITS[u][1] + 1]).then_inc(h1_ready, 1)

            def second_relu(u):
                act.wait_ge(h2_psum, u + 1)
                if u >= 2:
                    act.wait_ge(h2c_ready, u - 1)
                nc.scalar.activation(H2[:, u % 2, :], ps[:, 2 + u % 2, :], ACT.Relu,
                                     bias=cst("b2")[:, UNITS[u][1]:UNITS[u][1] + 1]).then_inc(h2_ready, 1)

            first_relu(0)
            gate(1)
            for u in range(len(UNITS)):
                if u + 1 < len(UNITS):
                    first_relu(u + 1)
                second_relu(u)
                if u == 0:
                    square(1, 3)
                if u == 1:
                    save_x2t(1)
                if u == 2:
                    router_hidden(1)
                if u == 3:
                    router_exp(1, 1)
                    router_exp(1, 2)
                if u == 5:
                    save_cwt(1)

        @block.vector
        def _(dve):
            steps = [0]

            def step(ins):
                steps[0] += 1
                ins.then_inc(dve_step, 1)
                dve.wait_ge(dve_step, steps[0])

            def over_c(k, b):
                return small[:, k, b].unsqueeze(2).to_broadcast([P, size(b), C])

            def over_b(ap, b):
                return ap.unsqueeze(1).to_broadcast([P, size(b), C])

            def over_e(k, b):
                return small[:, k, b].unsqueeze(2).to_broadcast([P, size(b), NE])

            def sum_c(source, b):
                return nc.vector.tensor_reduce(small[:, 0, b], source, AX.X, ALU.add)

            def conv_source(n):
                return conv_psum(0).rearrange("p (b c) -> p b c", c=C) if n == 0 else h[:, EARLY[1], :]

            def save_conv():
                dve.wait_ge(conv_done[1], 1)
                nc.vector.tensor_tensor(h[:, EARLY[1], :], conv_psum(1).rearrange("p (b c) -> p b c", c=C),
                                        over_b(rw("conv_b")[:, 0:C], EARLY[1]), ALU.add).then_inc(conv_saved, 1)

            def conv_sum(n):
                dve.wait_ge(conv_done[0] if n == 0 else conv_saved, 1)
                sum_c(conv_source(n), EARLY[n]).then_inc(sum_in[n], 1)

            def conv_centre(n):
                b = EARLY[n]
                dve.wait_ge(sum_out[n], 1)
                step(nc.vector.tensor_scalar(small[:, 3, b], ps[:, 2, b], 1.0 / (T * C), None, ALU.mult))
                nc.vector.tensor_tensor(tmp[:, b, :], conv_source(n), over_c(3, b), ALU.subtract).then_inc(centred[n], 1)

            def conv_square_sum(n):
                dve.wait_ge(squared[n], 1)
                sum_c(tmp2[:, EARLY[n], :], EARLY[n]).then_inc(sum_in[n], 1)

            def conv_variance(n):
                b = EARLY[n]
                dve.wait_ge(sum_out[n], 2)
                nc.vector.tensor_scalar(small[:, 1, b], ps[:, 2, NB + b.start:NB + b.stop], 1.0 / (T * C), CONV_EPS,
                                        ALU.mult, ALU.add).then_inc(var_ready[n], 1)

            def affine(n, part):
                b = EARLY[n]
                if part == 0:
                    dve.wait_ge(root_ready[n], 1)
                    step(nc.vector.tensor_tensor(h[:, b, :], over_b(rw("gamma"), b), over_c(5, b), ALU.mult))
                if part == 1:
                    step(nc.vector.tensor_tensor(tmp[:, b, :], tmp[:, b, :], h[:, b, :], ALU.mult))
                if part == 2:
                    nc.vector.tensor_tensor(tmp[:, b, :], tmp[:, b, :], over_b(rw("beta"), b),
                                            ALU.add).then_inc(yn_ready[n], 1)
                    dve.wait_ge(yn_ready[n], 1)

            def prelu(n, part):
                b = EARLY[n]
                if part == 0:
                    step(nc.vector.scalar_tensor_tensor(out=h[:, b, :], in0=tmp[:, b, :], scalar=0.0,
                                                        in1=over_b(rw("alpha"), b), op0=ALU.min, op1=ALU.mult))
                else:
                    dve.wait_ge(pos_ready[n], 1)
                    step(nc.vector.tensor_tensor(h[:, b, :], h[:, b, :], tmp2[:, b, :], ALU.add))

            def norm_mean(b):
                step(sum_c(h[:, b, :], b))
                step(nc.vector.tensor_scalar(small[:, 4, b], small[:, 0, b], 1.0 / C, None, ALU.mult))

            def norm_centre(n, b):
                nc.vector.tensor_tensor(tmp[:, b, :], h[:, b, :], over_c(4, b), ALU.subtract).then_inc(centred[n], 1)

            def norm_variance(n, turn):
                b = (EARLY, EARLY, LATE)[turn - 1][n]
                dve.wait_ge(squared[n], turn)
                step(sum_c(tmp2[:, b, :], b))
                nc.vector.tensor_scalar(small[:, 1, b], small[:, 0, b], 1.0 / C, LN_EPS,
                                        ALU.mult, ALU.add).then_inc(var_ready[n], 1)

            def norm_scale(n, i):
                b = EARLY[n]
                dve.wait_ge(root_ready[n], 2)
                nc.vector.tensor_tensor(xn2x[:, b, i, :], tmp[:, b, :], over_c(5, b), ALU.mult).then_inc(xn_ready[n], 1)

            def negate_x(n):
                for b in (EARLY[0],) if n == 0 else halves(EARLY[1]):
                    dve.wait_ge(xt_ready[n], (1, XT_BANKS)[n] if b.stop in (BG, NB) else 2)
                    for parity in range(2):
                        rows = slice(C * parity, C * parity + C)
                        src = XT[rows, b, :].rearrange("p b (g j i) -> p i b j g", g=TQ, i=2)[:, parity, :, :, :]
                        nc.vector.tensor_scalar(neg_x[rows, b, :, :], src, -1.0, None,
                                                ALU.mult).then_inc(neg_x_ready[n], 1)

            def save_xw(n):
                b = EARLY[n]
                dve.wait_ge(xw_psum[n], 1)
                nc.vector.tensor_copy(flat(neg_xw[:, b, :]), ps[:, 4, 0:size(b) * NH]).then_inc(xw_ready[n], 1)

            def save_q(G, turns=(0, 1)):
                for turn in turns:
                    dve.wait_ge(qp_ready, G * 2 + (turn + 1))
                    for bank in range(2):
                        for k in range(2):
                            hd = 4 * bank + 2 * turn + k
                            ins = nc.vector.tensor_scalar(
                                qn[:, hd, :, :],
                                ps[:, 4 + 2 * turn + bank, k * GC:(k + 1) * GC].rearrange("p (b t) -> p b t", b=BG),
                                cst("bq")[:, hd:hd + 1], inv_wk[:, hd:hd + 1], ALU.add, ALU.mult)
                    ins.then_inc(q_ready, 1)

            def pieces(G, J, halves=(0, 1)):
                for half in halves:
                    dve.wait_ge(half_free, G * NHALF + J * 2 + (half + 1))
                    for g, b in PIECES:
                        if (g, b) not in ACT_PIECES:
                            piece = relu_piece(nc.vector, G, J, half, g, b)
                    piece.then_inc(dve_half, 1)

            def subtract_first(G, bank):
                dve.wait_ge(first_part, G + 1)
                for to in (rest, opening):
                    ins = nc.vector.scalar_tensor_tensor(out=to[64:P, :], in0=ps[64:P, bank, 0:GC],
                                                         scalar=sum_b[64:P, :], in1=opening[64:P, :], op0=ALU.add,
                                                         op1=ALU.subtract)
                ins.then_inc(rest_ready, 1)

            def attention(G, last):
                if not last:
                    dve.wait_ge(act_half, G * NHALF + NHALF)
                    save_q(G + 1)
                dve.wait_ge(e_ready, G * BANKS + BANKS)
                nc.vector.tensor_scalar(den1[:], den[:], 1.0, None, ALU.add).then_inc(norm_step, 1)
                dve.wait_ge(norm_step, G * 2 + 1)
                nc.vector.reciprocal(rden[:], den1[:]).then_inc(norm_step, 1)
                dve.wait_ge(norm_step, G * 2 + 2)
                for k in range(BANKS):
                    hs = slice(HEADS_PER_BANK * k, HEADS_PER_BANK * (k + 1))
                    nc.vector.tensor_tensor(A[:, hs, :, :], A[:, hs, :, :],
                                            rden[:, hs, :].unsqueeze(3).to_broadcast([P, HEADS_PER_BANK, BG, T]),
                                            ALU.mult).then_inc(a_ready, 1)
                    if k == 1:
                        dve.wait_ge(vp_ready, G * BG + (BG + 1))
                        nc.vector.tensor_copy(V[:, 0, :, :], ps[:, 4:6, :]).then_inc(v0_ready, 1)
                if not last:
                    subtract_first(G + 1, 0)
                    dve.wait_ge(q_ready, G * 2 + 4)
                    pieces(G + 1, 0)

            def save_o(G):
                dve.wait_ge(o_done, G + 1)
                nc.vector.tensor_copy(flat(OT[:])[:, bass.ds(G * T, T)], ps[:, 6, 0:T]).then_inc(o_saved, 1)

            def gated(n):
                b = LATE[n]
                dve.wait_ge(gate_ready[n], 1)
                nc.vector.scalar_tensor_tensor(out=flat(tmp[:, b, :]), in0=flat(tmp2[:, b, :]), scalar=1.0,
                                               in1=flat(OT[:, gsl(b), :]), op0=ALU.add,
                                               op1=ALU.mult).then_inc(y_ready[n], 1)

            def add_residual(n):
                b = LATE[n]
                dve.wait_ge(base_ready, 1)
                dve.wait_ge(fan_done[n], 1)
                step(nc.vector.scalar_tensor_tensor(out=flat(h[:, b, :]), in0=late_psum(n, FAN_BANK), scalar=0.5,
                                                    in1=flat(base[:, b, :]), op0=ALU.mult, op1=ALU.add))

            def second_scale(n):
                b = LATE[n]
                dve.wait_ge(root_ready[n], 3)
                nc.vector.tensor_tensor(tmp[:, b, :], tmp[:, b, :], over_c(5, b), ALU.mult).then_inc(x2_ready[n], 1)

            def router_in(n):
                b = LATE[n]
                dve.wait_ge(logit_psum[n], 1)
                nc.vector.tensor_tensor(rt[:, 4, b], ps[:, 7, 0:size(b) * NE].rearrange("p (b e) -> p b e", e=NE),
                                        rw("rb2").unsqueeze(1).to_broadcast([P, size(b), NE]),
                                        ALU.add).then_inc(logit_read, 1)
                dve.wait_ge(logit_read, n + 1)
                step(nc.vector.tensor_reduce(small[:, 6, b], rt[:, 4, b], AX.X, ALU.max))
                nc.vector.tensor_tensor(rt[:, 0, b], rt[:, 4, b], over_e(6, b), ALU.subtract).then_inc(exp_in[n], 1)

            def router_out(n):
                b = LATE[n]
                g = gsl(b)
                r = rt[:, :, b, :]
                rank_a, rank_b = rank[:, 0, b], rank[:, 1, b]
                dve.wait_ge(exp_out[n], 1)
                step(nc.vector.tensor_reduce(small[:, 6, b], r[:, 1], AX.X, ALU.add))
                step(nc.vector.reciprocal(small[:, 7, b], small[:, 6, b]))
                nc.vector.tensor_tensor(r[:, 2], r[:, 1], over_e(7, b), ALU.mult).then_inc(exp_in[n], 1)
                dve.wait_ge(exp_in[n], 2)
                shape = [P, size(b), NE, NE]
                mine = r[:, 2].unsqueeze(3).to_broadcast(shape)
                other = r[:, 2].unsqueeze(2).to_broadcast(shape)
                lower = rw("lower").rearrange("p (e f) -> p e f", e=NE).unsqueeze(1).to_broadcast(shape)
                step(nc.vector.tensor_tensor(rank_a, other, mine, ALU.is_equal))
                step(nc.vector.tensor_tensor(rank_a, rank_a, lower, ALU.mult))
                step(nc.vector.tensor_tensor(rank_b, other, mine, ALU.is_gt))
                step(nc.vector.tensor_tensor(rank_a, rank_a, rank_b, ALU.add))
                step(nc.vector.tensor_reduce(r[:, 5], rank_a, AX.X, ALU.add))
                step(nc.vector.tensor_scalar(r[:, 6], r[:, 5], 1.5, None, ALU.is_lt))
                dve.wait_ge(exp_out[n], 2)
                step(nc.vector.tensor_tensor(r[:, 6], r[:, 6], r[:, 3], ALU.mult))
                step(nc.vector.tensor_reduce(small[:, 6, b], r[:, 6], AX.X, ALU.add))
                step(nc.vector.reciprocal(small[:, 7, b], small[:, 6, b]))
                step(nc.vector.tensor_tensor(r[:, 7], r[:, 6], over_e(7, b), ALU.mult))
                both = r[:, 7].rearrange("p (g i) e -> p g (i e)", i=BG)
                part = part_b[:].rearrange("p (g n) -> p g n", g=NG)[:, g, :]
                step(nc.vector.tensor_copy(part, both))
                step(nc.vector.tensor_copy(cw[:, g, 0, :], part))
                step(nc.vector.tensor_tensor(both, both, cw[:, g, 0, :], ALU.subtract))
                step(nc.vector.tensor_copy(part, both))
                step(nc.vector.tensor_copy(cw[:, g, 1, :], part))
                nc.vector.tensor_tensor(cw[:, g, 2, :], both, cw[:, g, 1, :], ALU.subtract).then_inc(cw_ready[n], 1)

            def weigh(u):
                dve.wait_ge(h2_ready, u + 1)
                if u >= 2:
                    dve.wait_ge(y_psum, u - 1)
                nc.vector.tensor_tensor(H2c[:, u % 2, :], H2[:, u % 2, :], ps[:, 4 + u % 2, :],
                                        ALU.mult).then_inc(h2c_ready, 1)

            def finish(n):
                dve.wait_ge(y_psum, NE * (n + 1))
                b = slice(n * BG * GH, (n + 1) * BG * GH)
                nc.vector.tensor_tensor(flat(result[:, b, :]), flat(h[:, b, :]), ps[:, 6 + n, :],
                                        ALU.add).then_inc(result_ready, 1)

            dve.wait_ge(const_loaded, 16)
            for k in range(TAPS):
                ins = nc.vector.tensor_scalar(conv[:, k, :], ident, cst("conv_w")[:, k:k + 1], None, ALU.mult)
            ins.then_inc(conv_ready, 1)
            step(nc.vector.tensor_scalar(inv_wk[:], cst("wk"), -1.0, None, ALU.mult))
            step(nc.vector.tensor_tensor(abs_wk[:], cst("wk"), inv_wk[:], ALU.max))
            step(nc.vector.tensor_scalar(abs_wk[:], abs_wk[:], TINY, None, ALU.max))
            step(nc.vector.tensor_scalar(sgn_wk[:], cst("wk"), 0.0, 2.0, ALU.is_ge, ALU.mult))
            step(nc.vector.tensor_scalar(sgn_wk[:], sgn_wk[:], -1.0, None, ALU.add))
            step(nc.vector.reciprocal(inv_wk[:], abs_wk[:]))
            step(nc.vector.tensor_tensor(inv_wk[:], inv_wk[:], sgn_wk[:], ALU.mult))
            nc.vector.tensor_scalar(wk8[:], abs_wk[:], -0.125, None, ALU.mult).then_inc(wk_ready, 1)

            step(nc.vector.memset(sum_wq[:], 0.0))
            step(nc.vector.memset(sum_bq[:], 0.0))
            step(nc.vector.tensor_tensor(sum_bq[:, 0:NH], sgn_wk[:], cst("bq"), ALU.mult))
            step(nc.vector.tensor_scalar(sum_bq[:, 0:NH], sum_bq[:, 0:NH], -0.5, None, ALU.mult))
            dve.wait_ge(qv_loaded, 16)
            half_sgn_flat = half_sgn[:].rearrange("p m c -> p (m c)")
            step(nc.vector.tensor_scalar(half_sgn_flat, cst("wk_q"), 0.0, -1.0, ALU.is_ge, ALU.mult))
            step(nc.vector.tensor_scalar(half_sgn_flat, half_sgn_flat, 0.5, None, ALU.add))
            step(nc.vector.tensor_tensor(half_sgn[:], half_sgn[:], wq[:, :, 0:C], ALU.mult))
            step(nc.vector.tensor_reduce(sum_q[:], half_sgn[:], AX.X, ALU.add))
            for at in PART_ROWS:
                for i in range(2):
                    rows_i = slice(C * i, C * i + C)
                    ins = nc.vector.tensor_copy(sum_wq[rows_i, at + 4 * i:at + 4 * i + 4], sum_q[rows_i, :])
                if at:
                    ins = nc.vector.tensor_copy(sum_bq[:, at:at + NH], sum_bq[:, 0:NH])
            ins.then_inc(sums_ready, 1)
            dve.wait_ge(rows_loaded, 16)
            conv_sum(0)
            conv_centre(0)
            conv_square_sum(0)
            conv_variance(0)
            dve.wait_ge(sum_b_psum, 1)
            nc.vector.tensor_copy(sum_b[:], ps[:, 3, GC:GC + 1]).then_inc(sum_b_ready, 1)
            for part in range(3):
                affine(0, part)
            for part in range(2):
                prelu(0, part)
            norm_mean(EARLY[0])
            norm_centre(0, EARLY[0])
            norm_variance(0, 2)
            for i in range(2):
                norm_scale(0, i)
            save_conv()
            conv_sum(1)
            negate_x(0)
            dve.wait_ge(sum_b_ready, 1)
            subtract_first(0, 3)
            conv_centre(1)
            save_q(0, (0,))
            conv_square_sum(1)
            save_q(0, (1,))
            conv_variance(1)
            dve.wait_ge(q_ready, 2)
            for k in range(NHALF):
                pieces(0, k // 2, (k % 2,))
                if k == 0:
                    save_xw(0)
                if k < 3:
                    affine(1, k)
                if k == 3:
                    prelu(1, 0)
                if k == 4:
                    prelu(1, 1)
                if k == 5:
                    norm_mean(EARLY[1])
                if k == 6:
                    norm_centre(1, EARLY[1])
                if k == 8:
                    norm_variance(1, 2)
                if k == 10:
                    norm_scale(1, 0)
                if k == 11:
                    norm_scale(1, 1)
            negate_x(1)
            save_xw(1)
            attention(0, False)
            save_o(0)
            with dve.Fori(1, NG - 1) as G:
                with dve.Fori(1, STEPS) as J:
                    pieces(G, J)
                attention(G, False)
                save_o(G)
            for k in range(2, NHALF):
                pieces(NG - 1, k // 2, (k % 2,))
                if k == 2:
                    gated(0)
                if k == 4:
                    add_residual(0)
                if k == 5:
                    norm_mean(LATE[0])
                if k == 6:
                    norm_centre(0, LATE[0])
                if k == 8:
                    norm_variance(0, 3)
                if k == 10:
                    second_scale(0)
            router_in(0)
            router_out(0)
            attention(NG - 1, True)
            save_o(NG - 1)
            gated(1)
            add_residual(1)
            norm_mean(LATE[1])
            norm_centre(1, LATE[1])
            for u in range(len(UNITS)):
                weigh(u)
                if u == 0:
                    norm_variance(1, 3)
                    second_scale(1)
                if u == 2:
                    router_in(1)
                if u == 3:
                    router_out(1)
                if u == 7:
                    finish(0)
            finish(1)

        @block.tensor
        def _(pe):
            pe.sem_inc(half_free, 2)
            pe.sem_inc(vp_ready, BG)
            pe.sem_inc(o_saved, 1)

            def convolve(g):
                for k, (first, _end) in enumerate(LOADS):
                    if g == first:
                        pe.wait_ge(x_loaded[k], 16)
                out_ap = conv_psum(0) if g == 0 else conv_psum(1)[:, (g - 1) * P:g * P]
                for k in range(TAPS):
                    ins = nc.tensor.matmul(out_ap, xc[:, g, k:k + T_IN:2],
                                           conv[:, k, :], start=(k == 0 and g in (1, 1 + 512 // P)),
                                           stop=(k == TAPS - 1), skip_group_check=True)
                if g in (0, NG - 1):
                    ins.then_inc(conv_done[min(g, 1)], 1)

            def sum_tokens(n, turn):
                pe.wait_ge(sum_in[n], turn + 1)
                b = EARLY[n]
                nc.tensor.matmul(ps[:, 2, NB * turn + b.start:NB * turn + b.stop], ones[:], small[:, 0, b],
                                 start=True, stop=True, skip_group_check=True).then_inc(sum_out[n], 1)

            def transpose_x(n):
                pe.wait_ge(xn_ready[n], 2)
                for m in range(size(EARLY[n])):
                    ins = nc.tensor.transpose(ps[:, XT_BANK[n] + m // 4, (m % 4) * T:(m % 4 + 1) * T],
                                              xn2x[:, EARLY[n].start + m, :, :].rearrange("p i c -> p (i c)"), ident)
                ins.then_inc(xt_psum[n], 1)

            def weigh_x(n):
                pe.wait_ge(xt_ready[n], (1, XT_BANKS)[n])
                for b in range(size(EARLY[n])):
                    ins = nc.tensor.matmul(ps[:, 4, b * NH:(b + 1) * NH], XT[0:C, EARLY[n].start + b, :], wk8[0:C, :],
                                           start=(b == 0), stop=True, skip_group_check=True)
                ins.then_inc(xw_psum[n], 1)

            def project_q(x, turns=(0, 1)):
                for turn in turns:
                    for k in range(2):
                        for half in range(2):
                            rows = slice(C * half, C * half + C)
                            ins = nc.tensor.matmul(ps[:, 4 + 2 * turn + half, k * GC:(k + 1) * GC],
                                                   wq[rows, 2 * turn + k, :], x[rows, :, :],
                                                   start=(k == 0), stop=True, skip_group_check=True)
                    ins.then_inc(qp_ready, 1)

            def sum_opening(x, bank):
                nc.tensor.matmul(ps[:, bank, 0:GC], sum_wq[:], x, start=True, stop=True,
                                 skip_group_check=True).then_inc(qsum_psum, 1)

            def start_distances(G):
                pe.wait_ge(opening_ready, G + 1)
                for hd in range(NH):
                    nc.tensor.matmul(R[:, hd, :], head_row[:, hd, :], opening[:],
                                     start=(hd % HEADS_PER_BANK == 0), stop=False, skip_group_check=True)

            def distances(G, J, halves=(0, 1)):
                for half in halves:
                    pe.wait_ge(win_ready, G * NHALF + J * 2 + (half + 1))
                    pe.wait_ge(dve_half, G * NHALF + J * 2 + (half + 1))
                    pe.wait_ge(act_half, G * NHALF + J * 2 + (half + 1))
                    for hd in range(NH):
                        for g in range(TQ):
                            ins = nc.tensor.matmul(R[32 * g:32 * g + 32, hd, :], window[:, half, hd, :],
                                                   D[:, half, g, hd * GC:(hd + 1) * GC],
                                                   start=False, stop=False, skip_group_check=True,
                                                   tile_position=(0, 32 * g))
                    ins.then_inc(half_free, 1)

            def attention(G, last):
                pe.wait_ge(x_copied, G + 1)
                pe.wait_ge(o_saved, G + 1)
                if not last:
                    project_q(x_next)
                    pe.wait_ge(e_ready, G * BANKS + 1)
                    sum_opening(x_next[:], 0)
                for b in range(BG):
                    if last:
                        pe.wait_ge(q_ready, G * 2 + 2)
                    else:
                        pe.wait_ge(q_ready, G * 2 + (3 + b))
                    for half in range(2):
                        rows = slice(C * half, C * half + C)
                        nc.tensor.matmul(ps[:, 4 + 2 * b + half, :], head_row[:, 0, :],
                                         bv_parts[:, 512 * half:512 * half + 512], start=True, stop=False,
                                         skip_group_check=True)
                        ins = nc.tensor.matmul(ps[:, 4 + 2 * b + half, :], x_now[rows, b, :], wv[rows, :],
                                               start=False, stop=True, skip_group_check=True)
                    ins.then_inc(vp_ready, 1)
                if last:
                    pe.wait_ge(e_ready, G * BANKS + 2)
                    first_layer(0)
                    first_layer(1)
                def transpose_a(k):
                    pe.wait_ge(a_ready, G * BANKS + (k + 1))
                    if k >= 2:
                        pe.wait_ge(v0_ready, G + 1)
                    for n in range(HEADS_PER_BANK * BG):
                        ins = nc.tensor.transpose(ps[:, AT_BANK + k, n * T:(n + 1) * T],
                                                  A[:, 2 * k + n // 2, n % 2, :], ident)
                    ins.then_inc(tp_ready, 1)

                for k in range(BANKS):
                    transpose_a(k)
                pe.wait_ge(v0_ready, G + 1)
                pe.wait_ge(v1_ready, G + 1)
                for k in range(BANKS):
                    pe.wait_ge(at_ready, G * BANKS + (k + 1))
                    if last and k == 2:
                        transpose_cw(0)
                    for hd in range(HEADS_PER_BANK * k, HEADS_PER_BANK * (k + 1)):
                        for d in range(2):
                            for b in range(BG):
                                ins = nc.tensor.matmul(ps[C * b:C * b + C, 6, 0:T],
                                                       V[:, b, d, hd * C:(hd + 1) * C], (AT, A)[d][:, hd, b, :],
                                                       start=(hd == 0 and d == 0), stop=(hd == NH - 1 and d == 1),
                                                       skip_group_check=True)
                ins.then_inc(o_done, 1)
                if not last:
                    pe.wait_ge(e_ready, G * BANKS + BANKS)
                    start_distances(G + 1)

            def project_y(n):
                pe.wait_ge(const2_loaded, 16)
                pe.wait_ge(y_ready[n], 1)
                for g in groups(LATE[n]):
                    at = g - gsl(LATE[n]).start
                    ins = nc.tensor.matmul(late_psum(n, FAN_BANK)[:, at * P:(at + 1) * P],
                                           flat(tmp[:])[:, g * T:(g + 1) * T], cst("fan"),
                                           start=(at % GH == 0), stop=True, skip_group_check=True)
                ins.then_inc(fan_done[n], 1)

            def transpose_x2(n):
                pe.wait_ge(x2_ready[n], 1)
                for g in groups(LATE[n]):
                    at = g - gsl(LATE[n]).start
                    ins = nc.tensor.transpose(late_psum(n, X2T_BANK)[:, at * P:(at + 1) * P],
                                              flat(tmp[:])[:, g * T:(g + 1) * T], ident)
                ins.then_inc(x2t_psum[n], 1)

            def router_first(n):
                pe.wait_ge(x2t_ready[n], 1)
                for g in groups(LATE[n])[::GH]:
                    at, end = g - gsl(LATE[n]).start, min(g + GH, gsl(LATE[n]).stop)
                    ins = nc.tensor.matmul(late_psum(n, RH_BANK)[0:BG * RH, at * T:(at + end - g) * T], cst("rw1"),
                                           X2T[:, g:end, :], start=True, stop=True)
                ins.then_inc(rh_psum[n], 1)

            def router_second(n):
                pe.wait_ge(rh_ready[n], 1)
                for g in groups(LATE[n]):
                    at = g - gsl(LATE[n]).start
                    ins = nc.tensor.matmul(ps[:, 7, at * BG * NE:(at + 1) * BG * NE], rhT[0:BG * RH, g, :],
                                           cst("rw2")[0:BG * RH, :], start=(at == 0), stop=True, skip_group_check=True)
                ins.then_inc(logit_psum[n], 1)

            def transpose_cw(n):
                pe.wait_ge(cw_ready[n], 1)
                for g in groups(LATE[n]):
                    at = g - gsl(LATE[n]).start
                    ins = nc.tensor.transpose(late_psum(n, CWT_BANK)[0:CK, at * T:(at + 1) * T], flat(cw[:, g, :, :]),
                                              ident)
                ins.then_inc(cwt_psum[n], 1)

            def first_layer(u):
                n, e = UNITS[u]
                if u >= 2:
                    pe.wait_ge(h1_ready, u - 1)
                if e == 0:
                    pe.wait_ge(x2t_ready[n], 1)
                nc.tensor.matmul(ps[:, u % 2, :], cst("w1")[:, e * P:(e + 1) * P], X2T[:, unit(n), :],
                                 start=True, stop=True).then_inc(h1_psum, 1)

            def second_layer(u):
                n, e = UNITS[u]
                if u >= 2:
                    pe.wait_ge(h2c_ready, u - 1)
                if e == 0:
                    pe.wait_ge(cwt_ready[n], 2)
                nc.tensor.matmul(ps[:, 4 + u % 2, :], pick_b[0:CK, e * P:(e + 1) * P], cwT_b[0:CK, unit(n), :],
                                 start=True, stop=True)
                pe.wait_ge(h1_ready, u + 1)
                nc.tensor.matmul(ps[:, 2 + u % 2, :], cst("w2")[:, e * P:(e + 1) * P], H1[:, u % 2, :],
                                 start=True, stop=True).then_inc(h2_psum, 1)

            def third_layer(u):
                n, e = UNITS[u]
                if e == 0:
                    for g in range(GH):
                        nc.tensor.matmul(ps[:, 6 + n, g * P:(g + 1) * P], cwT[0:CK, n * GH + g, :],
                                         cst("b3")[0:CK, :], start=(g == 0), stop=False, skip_group_check=True)
                pe.wait_ge(h2c_ready, u + 1)
                for g in range(GH):
                    ins = nc.tensor.matmul(ps[:, 6 + n, g * P:(g + 1) * P], H2c[:, u % 2, g * T:(g + 1) * T],
                                           cst("w3")[:, e * P:(e + 1) * P], start=False, stop=(e == NE - 1),
                                           skip_group_check=True)
                ins.then_inc(y_psum, 1)

            pe.wait_ge(pool_step, 1)
            pe.wait_ge(rows_loaded, 16)
            nc.tensor.matmul(ps[:, 4, 0:BG * C], ones[0:1, :], rw("conv_b")[0:1, 0:BG * C], start=True, stop=False,
                             skip_group_check=True)
            pe.wait_ge(conv_ready, 1)
            convolve(0)
            convolve(1)
            sum_tokens(0, 0)
            convolve(2)
            sum_tokens(0, 1)
            pe.wait_ge(sums_ready, 1)
            nc.tensor.matmul(ps[:, 3, GC:GC + 1], sum_bq[0:C, :], ones[0:C, 0:1], start=True, stop=True,
                             skip_group_check=True).then_inc(sum_b_psum, 1)
            for g in range(3, NG):
                convolve(g)
            transpose_x(0)
            pe.wait_ge(xt_ready[0], 1)
            pe.wait_ge(qv_loaded, 16)
            pe.wait_ge(sum_b_ready, 1)
            sum_opening(XT[:, 0:BG, :], 3)
            project_q(XT[:, 0:BG, :], (0,))
            sum_tokens(1, 0)
            project_q(XT[:, 0:BG, :], (1,))
            sum_tokens(1, 1)
            pe.wait_ge(q_ready, 1)
            weigh_x(0)
            pe.wait_ge(rows_ready, 1 + PARTS)
            pe.wait_ge(conv_saved, 1)
            pe.wait_ge(var_ready[1], 1)
            start_distances(0)
            for k in range(NHALF):
                distances(0, k // 2, (k % 2,))
                if k == 12:
                    pe.wait_ge(xw_ready[0], 1)
                    transpose_x(1)
            weigh_x(1)
            pe.wait_ge(xw_ready[1], 1)
            pe.wait_ge(bv_ready, 1)
            attention(0, False)
            with pe.Fori(1, NG - 1) as G:
                with pe.Fori(0, STEPS) as J:
                    distances(G, J)
                attention(G, False)
            for k in range(NHALF):
                distances(NG - 1, k // 2, (k % 2,))
                if k == 2:
                    pe.wait_ge(o_saved, NG)
                    project_y(0)
                if k == 10:
                    transpose_x2(0)
                if k == 12:
                    router_first(0)
                if k == 14:
                    router_second(0)
            pe.wait_ge(logit_read, 1)
            attention(NG - 1, True)
            pe.wait_ge(pick_ready, 1)
            for u in range(len(UNITS) + 1):
                if 1 <= u and u + 1 < len(UNITS):
                    first_layer(u + 1)
                if u < len(UNITS):
                    second_layer(u)
                if u == 0:
                    project_y(1)
                if u >= 1:
                    third_layer(u - 1)
                if u == 1:
                    transpose_x2(1)
                if u == 2:
                    router_first(1)
                    router_second(1)
                if u == 5:
                    transpose_cw(1)


def _pack(inputs):
    import numpy as np

    g = {k: np.asarray(v) for k, v in inputs.items()}
    dt = g["x"].dtype
    x_t = np.zeros((BG, C, NG, X_ROWS), dt)
    x_t[:, :, :, 1:T_IN + 1] = g["x"].reshape(NG, BG, T_IN, C).transpose(1, 3, 0, 2)

    packed = [np.zeros((P, NCOLS), dt), np.zeros((P, NCOLS2), dt)]

    def put(name, rows, value):
        k, a, b = COLS[name]
        packed[k][rows, a:b] = value.reshape(value.shape[0], -1)

    def put_block(name, rows, n, i, value):
        k, a, _ = COLS[name]
        a += BG * value.shape[1] * n + value.shape[1] * i
        packed[k][rows, a:a + value.shape[1]] = value

    wqv_t = g["L0_attn_wqv_w"].T
    q_t = wqv_t[:, :NH * C].reshape(C, NH, 1, C)
    q_t = np.concatenate([q_t, q_t], axis=2)
    v_t = wqv_t[:, NH * C:]
    put("ident", slice(0, P), np.eye(P, dtype=dt))
    for i in range(BG):
        rows = slice(C * i, C * i + C)
        put("conv_w", rows, g["L0_tok_w"].reshape(TAPS, C).T)
        put("wk", rows, g["L0_attn_wk"].T)
        put("bq", rows, g["L0_attn_wqv_b"][:NH * C].reshape(NH, C).T)
        put("wq", rows, q_t[:, 4 * i:4 * i + 4])
        put("wk_q", rows, np.broadcast_to(g["L0_attn_wk"][4 * i:4 * i + 4].reshape(1, 4 * C), (C, 4 * C)))
        put("wv", rows, v_t[:, NH * C * i:NH * C * (i + 1)])
        put("b1", rows, g["L0_ffn_expert_b1"].T)
        put("b2", rows, g["L0_ffn_expert_b2"].T)
        put("rb1", slice(RH * i, RH * i + RH), g["L0_ffn_router_b1"].reshape(RH, 1))
        put_block("fan", rows, 0, i, g["L0_attn_fanin_w"].T)
        put_block("rw1", rows, 0, i, g["L0_ffn_router_w1"])
        put_block("rw2", slice(RH * i, RH * i + RH), 0, i, g["L0_ffn_router_w2"])
        for e in range(NE):
            put_block("w1", rows, e, i, g["L0_ffn_expert_w1"][e])
            put_block("w2", rows, e, i, g["L0_ffn_expert_w2"][e])
            put_block("w3", rows, e, i, g["L0_ffn_expert_w3"][e])
            for part in range(PARTS):
                one = (part * BG + i) * NE + e
                put_block("pick", slice(one, one + 1), e, i, np.ones((1, C), dt))
        for part in range(PARTS):
            put_block("b3", slice((part * BG + i) * NE, (part * BG + i + 1) * NE), 0, i, g["L0_ffn_expert_b3"])

    lower = np.tril(np.ones((NE, NE), dt), -1)
    conv_b = g["L0_tok_b"]
    parts = {"conv_b": np.concatenate([conv_b] * (NB // 2)), "gamma": g["L0_tok_gamma"], "beta": g["L0_tok_beta"],
             "alpha": g["L0_tok_alpha"], "fan_b": g["L0_attn_fanin_b"], "bv": g["L0_attn_wqv_b"][NH * C:],
             "rb2": g["L0_ffn_router_b2"], "lower": lower}
    rows = np.concatenate([parts[name].reshape(-1) for name in ROWS]).reshape(NROWS)
    return {"x_t": x_t.reshape(P, NG, X_ROWS), "cols": packed[0], "cols2": packed[1], "rows": rows}


def kernel(**inputs):
    import concourse.bacc as _bacc
    from concourse.bass_utils import run_bass_kernel_spmd as _run

    arrays = _pack(inputs)
    nc = _bacc.Bacc("TRN2", target_bir_lowering=False, num_devices=1)
    args = [nc.dram_tensor(name, a.shape, mybir.dt.from_np(a.dtype), kind="ExternalInput").ap()
            for name, a in arrays.items()]
    out = nc.dram_tensor("out", (NB, T, C), F32, kind="ExternalOutput").ap()
    build(nc, *args, out)
    return _run(nc, [arrays], core_ids=[0]).results[0]["out"]
```
